# Optimizing a Trainium2 kernel written in Bass

```python
import numpy as np
import jax
import jax.numpy as jnp

def _softmax(x, axis=-1):
    return jax.nn.softmax(x, axis=axis)

def _gelu(x):
    return jax.nn.gelu(x, approximate=True)

def _silu(x):
    return jax.nn.silu(x)

def _sigmoid(x):
    return jax.nn.sigmoid(x)

def _layernorm(x, axis=-1, eps=1e-05):
    m = jnp.mean(x, axis=axis, keepdims=True)
    v = jnp.var(x, axis=axis, keepdims=True)
    return (x - m) / jnp.sqrt(v + eps)

def _scatter_add(tgt, idx, src, axis=0):
    return tgt.at[idx].add(src)

def _segment_sum(src, seg, n):
    return jax.ops.segment_sum(src, seg, n)
kernel_name = 'mk_perceiver_d1_seqx_r2_53ed5f'

def setup_inputs(seed: int=0):
    np.random.seed(seed)
    _w = jnp.asarray

    def _rec_inputs():
        import jax
        import jax.numpy as jnp
        _rk = jax.random.key(seed)
        x = 7.22e-05 + 1 * jax.random.normal(jax.random.fold_in(_rk, 1), (8, 64, 512), jnp.float32)
        _lenS = 64 - jax.random.randint(jax.random.fold_in(_rk, 7), (8,), 0, max(1, 64 // 4) + 1, jnp.int32)
        _lenS2 = 1601 - jax.random.randint(jax.random.fold_in(_rk, 8), (8,), 0, max(1, 1601 // 4) + 1, jnp.int32)
        _ctx_1024P = jax.random.normal(jax.random.fold_in(_rk, 11), (8, 16, 512), jnp.float32)
        _ctx_1024c = jax.random.dirichlet(jax.random.fold_in(_rk, 511), 0.3 * jnp.ones((16,), jnp.float32), (8, 1601))
        _ctx_1024t = jnp.einsum('bsk,bkd->bsd', _ctx_1024c, _ctx_1024P)
        _ctx_1024t = _ctx_1024t * jax.lax.rsqrt(jnp.mean(jnp.square(_ctx_1024t)) + 1e-12) * 0.953939
        ctx_1024 = 4.13588e-05 + 0.999923 * (_ctx_1024t + 0.3 * jax.random.normal(jax.random.fold_in(_rk, 611), (8, 1601, 512), jnp.float32))
        return (x, ctx_1024)
    x, ctx_1024 = _rec_inputs()

    def _L0_xattn_setup():
        import jax, jax.numpy as jnp
        import numpy as np
        D_MODEL = 512
        NHEAD = 16
        key = jax.random.key(seed)
        ks = jax.random.split(key, 11)
        B, S, D = (4, 1024, D_MODEL)
        scale = 1.0 / np.sqrt(D)
        inp = {'q': jax.random.normal(ks[0], (B, S, D), jnp.float32), 'k': jax.random.normal(ks[1], (B, S, D), jnp.float32), 'v': jax.random.normal(ks[2], (B, S, D), jnp.float32), 'Wq': jax.random.normal(ks[3], (D, D), jnp.float32) * scale, 'bq': jnp.zeros((D,), jnp.float32), 'Wk': jax.random.normal(ks[4], (D, D), jnp.float32) * scale, 'bk': jnp.zeros((D,), jnp.float32), 'Wv': jax.random.normal(ks[5], (D, D), jnp.float32) * scale, 'bv': jnp.zeros((D,), jnp.float32), 'Wo': jax.random.normal(ks[6], (D, D), jnp.float32) * scale, 'bo': jnp.zeros((D,), jnp.float32)}
        return inp
    _L0_xattn_all = _L0_xattn_setup()
    _L0_xattn_in = {k: v for k, v in _L0_xattn_all.items() if k in ('Wq', 'bq', 'Wk', 'bk', 'Wv', 'bv', 'Wo', 'bo')}
    del _L0_xattn_all

    def _L0_attn_setup():
        import jax, jax.numpy as jnp
        import numpy as np
        B, N, D, H = (4, 1024, 512, 8)
        HD = D // H
        TEMPER = 1.0
        LN_EPS = 1e-05

        def _leaky(x):
            return jnp.where(x > 0, x, 0.01 * x)
        key = jax.random.key(seed)
        ks = jax.random.split(key, 6)
        return {'h': jax.random.normal(ks[0], (B, N, D), dtype=jnp.float32), 'Wl': jax.random.normal(ks[1], (D, D), dtype=jnp.float32) * D ** (-0.5), 'Wr': jax.random.normal(ks[2], (D, D), dtype=jnp.float32) * D ** (-0.5), 'att_l': jax.random.normal(ks[3], (1, HD), dtype=jnp.float32) * HD ** (-0.5), 'att_r': jax.random.normal(ks[4], (1, HD), dtype=jnp.float32) * HD ** (-0.5), 'Wf': jax.random.normal(ks[5], (D, D), dtype=jnp.float32) * D ** (-0.5), 'ln_gamma': jnp.ones((D,), dtype=jnp.float32), 'ln_beta': jnp.zeros((D,), dtype=jnp.float32)}
    _L0_attn_all = _L0_attn_setup()
    _L0_attn_in = {k: v for k, v in _L0_attn_all.items() if k in ('Wl', 'Wr', 'att_l', 'att_r', 'Wf', 'ln_gamma', 'ln_beta')}
    del _L0_attn_all

    def _L0_ffn_setup():
        import jax, jax.numpy as jnp
        import numpy as np
        DIM = 512
        HIDDEN = 2048
        N_EXPERTS = 8
        K = 2
        TEMP = 1.0

        def _expert_ffn(xf, wa, ba, wb, bb):
            h = xf @ wa.T + ba
            h1, h2 = jnp.split(h, 2, axis=-1)
            h = jax.nn.silu(h1) * h2
            return h @ wb.T + bb
        key = jax.random.key(seed)
        ks = jax.random.split(key, 7)
        s = 0.02
        x = jax.random.normal(ks[0], (4, 1024, DIM), dtype=jnp.float32)
        router_w = jax.random.normal(ks[1], (N_EXPERTS, DIM), dtype=jnp.float32) * s
        router_b = jnp.zeros((N_EXPERTS,), dtype=jnp.float32)
        w1 = jax.random.normal(ks[2], (N_EXPERTS, 2 * HIDDEN, DIM), dtype=jnp.float32) * s
        b1 = jnp.zeros((N_EXPERTS, 2 * HIDDEN), dtype=jnp.float32)
        w2 = jax.random.normal(ks[3], (N_EXPERTS, DIM, HIDDEN), dtype=jnp.float32) * s
        b2 = jnp.zeros((N_EXPERTS, DIM), dtype=jnp.float32)
        return {'x': x, 'router_w': router_w, 'router_b': router_b, 'w1': w1, 'b1': b1, 'w2': w2, 'b2': b2}
    _L0_ffn_all = _L0_ffn_setup()
    _L0_ffn_in = {k: v for k, v in _L0_ffn_all.items() if k in ('router_w', 'router_b', 'w1', 'b1', 'w2', 'b2')}
    del _L0_ffn_all
    return {'x': x, 'ctx_1024': ctx_1024, 'L0_xattn_Wq': _L0_xattn_in['Wq'], 'L0_xattn_bq': _L0_xattn_in['bq'], 'L0_xattn_Wk': _L0_xattn_in['Wk'], 'L0_xattn_bk': _L0_xattn_in['bk'], 'L0_xattn_Wv': _L0_xattn_in['Wv'], 'L0_xattn_bv': _L0_xattn_in['bv'], 'L0_xattn_Wo': _L0_xattn_in['Wo'], 'L0_xattn_bo': _L0_xattn_in['bo'], 'L0_attn_Wl': _L0_attn_in['Wl'], 'L0_attn_Wr': _L0_attn_in['Wr'], 'L0_attn_att_l': _L0_attn_in['att_l'], 'L0_attn_att_r': _L0_attn_in['att_r'], 'L0_attn_Wf': _L0_attn_in['Wf'], 'L0_attn_ln_gamma': _L0_attn_in['ln_gamma'], 'L0_attn_ln_beta': _L0_attn_in['ln_beta'], 'L0_ffn_router_w': _L0_ffn_in['router_w'], 'L0_ffn_router_b': _L0_ffn_in['router_b'], 'L0_ffn_w1': _L0_ffn_in['w1'], 'L0_ffn_b1': _L0_ffn_in['b1'], 'L0_ffn_w2': _L0_ffn_in['w2'], 'L0_ffn_b2': _L0_ffn_in['b2']}

def reference(x, ctx_1024, L0_xattn_Wq, L0_xattn_bq, L0_xattn_Wk, L0_xattn_bk, L0_xattn_Wv, L0_xattn_bv, L0_xattn_Wo, L0_xattn_bo, L0_attn_Wl, L0_attn_Wr, L0_attn_att_l, L0_attn_att_r, L0_attn_Wf, L0_attn_ln_gamma, L0_attn_ln_beta, L0_ffn_router_w, L0_ffn_router_b, L0_ffn_w1, L0_ffn_b1, L0_ffn_w2, L0_ffn_b2):
    import jax
    import jax.numpy as jnp

    def _L0_xattn_ref(q, k, v, Wq, bq, Wk, bk, Wv, bv, Wo, bo):
        import jax, jax.numpy as jnp
        import numpy as np
        D_MODEL = 512
        NHEAD = 16
        qp = jnp.einsum('bsd,ed->bse', q, Wq) + bq
        kp = jnp.einsum('bsd,ed->bse', k, Wk) + bk
        vp = jnp.einsum('bsd,ed->bse', v, Wv) + bv
        scale = 1.0 / np.sqrt(D_MODEL / NHEAD)
        scores = jnp.einsum('bqd,bkd->bqk', qp, kp) * scale
        attn = jax.nn.softmax(scores, axis=-1)
        out = jnp.einsum('bqk,bkd->bqd', attn, vp)
        return jnp.einsum('bsd,ed->bse', out, Wo) + bo

    def _L0_attn_ref(h, Wl, Wr, att_l, att_r, Wf, ln_gamma, ln_beta):
        import jax, jax.numpy as jnp
        import numpy as np
        B, N, D, H = (4, 1024, 512, 8)
        HD = D // H
        TEMPER = 1.0
        LN_EPS = 1e-05

        def _leaky(x):
            return jnp.where(x > 0, x, 0.01 * x)
        b, n, d = h.shape
        fl = (h @ Wl.T).reshape(b, n, H, HD).transpose(0, 2, 1, 3)
        fr = (h @ Wr.T).reshape(b, n, H, HD).transpose(0, 2, 1, 3)
        sl = jnp.einsum('bhnd,d->bhn', _leaky(fl), att_l[0])
        sr = jnp.einsum('bhnd,d->bhn', _leaky(fr), att_r[0])
        score = (sl[:, :, :, None] + sr[:, :, None, :]) / TEMPER
        p = jax.nn.softmax(score, axis=-1)
        ctx = jnp.einsum('bhnm,bhmd->bhnd', p, fr)
        h_sa = ctx.transpose(0, 2, 1, 3).reshape(b, n, d)
        fh = h_sa @ Wf.T
        y = h + fh
        mu = jnp.mean(y, axis=-1, keepdims=True)
        var = jnp.mean(jnp.square(y - mu), axis=-1, keepdims=True)
        return (y - mu) * jax.lax.rsqrt(var + LN_EPS) * ln_gamma + ln_beta

    def _L0_ffn_ref(x, router_w, router_b, w1, b1, w2, b2):
        import jax, jax.numpy as jnp
        import numpy as np
        DIM = 512
        HIDDEN = 2048
        N_EXPERTS = 8
        K = 2
        TEMP = 1.0

        def _expert_ffn(xf, wa, ba, wb, bb):
            h = xf @ wa.T + ba
            h1, h2 = jnp.split(h, 2, axis=-1)
            h = jax.nn.silu(h1) * h2
            return h @ wb.T + bb
        b, t, d = x.shape
        logits = (x @ router_w.T + router_b) / TEMP
        topk_val, topk_idx = jax.lax.top_k(logits, K)
        weights = jax.nn.softmax(topk_val, axis=-1)
        xf = x.reshape(-1, d)
        outs = jax.vmap(_expert_ffn, in_axes=(None, 0, 0, 0, 0))(xf, w1, b1, w2, b2)
        outs = jnp.transpose(outs, (1, 0, 2))
        idx = topk_idx.reshape(-1, K)
        gathered = jnp.take_along_axis(outs, idx[:, :, None], axis=1)
        combined = (gathered * weights.reshape(-1, K, 1)).sum(axis=1)
        return combined.reshape(b, t, d)
    x = x + _L0_xattn_ref(_layernorm(x, axis=-1), ctx_1024, ctx_1024, L0_xattn_Wq, L0_xattn_bq, L0_xattn_Wk, L0_xattn_bk, L0_xattn_Wv, L0_xattn_bv, L0_xattn_Wo, L0_xattn_bo)
    x = x + _L0_attn_ref(_layernorm(x, axis=-1), L0_attn_Wl, L0_attn_Wr, L0_attn_att_l, L0_attn_att_r, L0_attn_Wf, L0_attn_ln_gamma, L0_attn_ln_beta)
    x = x + _L0_ffn_ref(_layernorm(x, axis=-1), L0_ffn_router_w, L0_ffn_router_b, L0_ffn_w1, L0_ffn_b1, L0_ffn_w2, L0_ffn_b2)
    return x

_drawn_inputs = setup_inputs


def setup_inputs(seed=0):
    import zlib

    import numpy as np

    out = dict(_drawn_inputs(seed))
    spreads = {'L0_xattn_bq': (0.0, 0.1),
     'L0_xattn_bk': (0.0, 0.8),
     'L0_xattn_bv': (0.0, 0.1),
     'L0_xattn_bo': (0.0, 0.1),
     'L0_attn_ln_gamma': (1.0, 0.2),
     'L0_attn_ln_beta': (0.0, 0.1),
     'L0_ffn_router_b': (0.0, 0.541),
     'L0_ffn_b1': (0.0, 0.8),
     'L0_ffn_b2': (0.0, 0.1)}
    factors = {'L0_attn_Wl': 8.0, 'L0_attn_att_l': 8.0}
    for name, (base, spread) in spreads.items():
        noise = np.random.default_rng([zlib.crc32(name.encode()), seed]).standard_normal(out[name].shape)
        drawn = base * np.exp(spread * noise) if base else spread * noise
        out[name] = jnp.asarray(drawn.astype(out[name].dtype))
    for name, factor in factors.items():
        out[name] = (out[name] * factor).astype(out[name].dtype)
    return out
```

```python
import concourse.bass as bass
from concourse import mybir
from contextlib import ExitStack

F32 = mybir.dt.float32
I32 = mybir.dt.int32
U32 = mybir.dt.uint32
ALU = mybir.AluOpType
ACT = mybir.ActivationFunctionType
AX = mybir.AxisListType

P = 128
B, S, D = 8, 64, 512
KEYS = 1601
TOK = B * S
T = TOK // P
KD = D // P
JF = KEYS // P
REST = KEYS - JF * P
J = JF + 1
H, HD = 8, 64
E, FF = 8, 2048
M2 = FF // P
W = 64
CH_MAX = 2 * TOK // W + E
PIECES = 4
MP = M2 // PIECES
LAG = 3
SCALE = 1.0 / float(D / 16) ** 0.5
EPS = 1e-5
LOWEST = -3.0e38


class Order:

    def __init__(self, eng, sem, base=0):
        self.eng, self.sem, self.base, self.n = eng, sem, base, 0

    def step(self, ins):
        self.n += 1
        ins.then_inc(self.sem, 1)
        return self.n

    def settle(self, n=None):
        self.eng.wait_ge(self.sem, self.base + (self.n if n is None else n))

    def link(self, ins):
        self.step(ins)
        self.settle()


def perceiver_layer(nc, x, ctx_in, wq, bq, wk, bk, wv, bv, wo, bo, wl, wr, att_l, att_r, wf, gamma, beta,
                    rw, rb, w1, b1, w2, b2, out):
    es = ExitStack()

    def sem(name):
        return es.enter_context(nc.semaphore(name))

    with es:
        NW1 = M2 * 2 * KD * P
        NW2 = M2 * D
        NARENA = 52400
        arena = es.enter_context(nc.sbuf_tensor("arena", [P, NARENA], F32))
        bank = [es.enter_context(nc.psum_tensor(f"bank{i}", [P, 512], F32)) for i in range(8)]
        base_i = es.enter_context(nc.sbuf_tensor("base_i", [P, E + 1], I32))
        dest_i = es.enter_context(nc.sbuf_tensor("dest_i", [P, 2, T], I32))
        from_i = es.enter_context(nc.sbuf_tensor("from_i", [P, 2, T], I32))
        rows_in = nc.dram_tensor("rows_in", [(CH_MAX + 2) * W, D], F32, kind="Internal").ap()
        rows_out = nc.dram_tensor("rows_out", [(CH_MAX + 2) * W, D], F32, kind="Internal").ap()

        def area(start, *shape):
            n = 1
            for s in shape:
                n *= s
            assert start + n <= NARENA
            v = arena[:, start:start + n]
            if len(shape) == 1:
                return v
            names = "abcd"[:len(shape)]
            return v.rearrange(f"p ({' '.join(names)}) -> p {' '.join(names)}",
                               **dict(zip(names[1:], shape[1:])))

        W1A, W2A, W1B = 0, NW1, NW1 + NW2
        w1buf = [area(W1A, M2, 2, KD, P), area(W1B, M2, 2, KD, P)]
        w2buf = area(W2A, M2, D)
        NCTX = J * D
        ctx = [area(i * NCTX, J, D) for i in range(2)]
        NRING = 4
        ctxT = [area(2 * NCTX + i * D, KD, P) for i in range(NRING)]
        assert 2 * NCTX + NRING * D <= W2A
        at = W2A
        wq_s = area(at, KD, D)
        wk_s = area(at + KD * D, KD, D)
        xnT = area(at + 2 * KD * D, KD, TOK)
        qT = area(at + 3 * KD * D, KD, TOK)
        NB = KD * D
        at = W1B
        wv_s, wo_s, wl_s, wr_s, wf_s = (area(at + i * NB, KD, D) for i in range(5))
        aT = area(at + 5 * NB, KD, TOK)
        qkT = area(at + 6 * NB, KD, TOK)
        vT = qkT
        hT = aT
        fr = wv_s.rearrange("p k d -> p (k d)").rearrange("p (t d) -> p t d", t=T)
        hsT = vT
        xT = hT
        att_tmp = area(at + 7 * NB, 4, 512)
        assert 8 * NB <= NW1
        at = W1B + NW1
        def take(*shape):
            nonlocal at
            v = area(at, *shape)
            n = 1
            for s in shape:
                n *= s
            at += n
            return v
        xres = take(T, D)
        xn = take(T, D)
        h_nat = xn
        ident = take(P)
        ones = take(P)
        same = take(P)
        below = take(P)
        place = take(S)
        bq_s, bk_s, bv_s = take(KD), take(KD), take(KD)
        iota = take(E)
        over = take(7)
        tri = take(E + 1, E)
        rb_s = take(E)
        rw_s = take(KD, E)
        attl_s, attr_s = take(HD), take(HD)
        stats, mv, rstd = take(T, 6), take(T, 2), take(T)
        half = take(1)
        b1_s = [take(2, M2) for _ in range(2)]
        b2_s = [take(KD) for _ in range(2)]
        gate = take(2, T)
        shared = at
        sc = take(J, S)
        pr = take(J, S)
        bkq = take(TOK)
        mx, mxr, dg, dsum, rec = take(S), take(1), take(S), take(S), take(S)
        bk_wide = area(W1B + 7 * NB, KD, P)
        bo_s = area(W1B + 7 * NB + D, D)
        endB = at
        at = shared
        lk = [take(D) for _ in range(2)]
        spread = [take(2, H, S) for _ in range(1)][0]
        gamma_s, beta_s = take(D), take(D)
        sl, sr, slm, srx = take(T, H), take(T, H), take(T, H), take(2)
        mxl = take(P)
        lg, eq, cand, oh1, oh2, lg2, both, rank = (take(T, E) for _ in range(8))
        top = take(2, T)
        idx, ew, wsum = take(T), take(T), take(T)
        dst_f = take(2, T)
        cnt, chs, basef = take(E), take(E), take(E + 1)
        cmp7, cmp9 = take(E, 7), take(E + 1, E)
        endC = at
        at = shared
        zeros = take(D)
        xg = take(D)[0:W, :]
        xgT = take(KD, W)
        act_s = [take(W) for _ in range(4)]
        hid = take(M2, W)
        yT = take(KD, W)
        yrow = take(D)[0:W, :]
        endD = at
        assert max(endB, endC, endD) <= NARENA, (endB, endC, endD)
        zeros = area(2 * NCTX + NRING * D, D)
        assert 2 * NCTX + (NRING + 1) * D <= W2A
        got = area(W1A, 2, T, D)

        x_in = sem("x_in")
        wqk_in = sem("wqk_in")
        small_in = sem("small_in")
        wide_in = sem("wide_in")
        ctx_in_s = [sem(f"ctx_in{i}") for i in range(2)]
        ctx_rest = [sem(f"ctx_rest{i}") for i in range(2)]
        wc_in = sem("wc_in")
        const_ok = sem("const_ok")
        p_order, v_order, a_order = sem("p_order"), sem("v_order"), sem("a_order")
        rstd_ok = sem("rstd_ok")
        var_ok = sem("var_ok")
        xn_ok = sem("xn_ok")
        xb_ok = sem("xb_ok")
        xt_done, xnT_ok = sem("xt_done"), sem("xnT_ok")
        q_done, qT_ok = sem("q_done"), sem("qT_ok")
        qk_done, qkT_ok = sem("qk_done"), sem("qkT_ok")
        bkw_ok = sem("bkw_ok")
        bkq_done, bkq_ok = sem("bkq_done"), sem("bkq_ok")
        turn_done, turn_act, turn_dve = sem("turn_done"), sem("turn_act"), sem("turn_dve")
        sc_done, sc_out = sem("sc_done"), sem("sc_out")
        mx_ok, mxT_done, dg_ok, mxb_done = sem("mx_ok"), sem("mxT_done"), sem("dg_ok"), sem("mxb_done")
        sub_ok, exp_ok, dsum_ok, den_done = sem("sub_ok"), sem("exp_ok"), sem("dsum_ok"), sem("den_done")
        av_done, aT_ok = sem("av_done"), sem("aT_ok")
        sc_order, mxr_ok, rec_ok = sem("sc_order"), sem("mxr_ok"), sem("rec_ok")
        v_done, vT_ok = sem("v_done"), sem("vT_ok")
        o_done, x1_ok = sem("o_done"), sem("x1_ok")
        h_ok, ht_done, hT_ok = sem("h_ok"), sem("ht_done"), sem("hT_ok")
        f_done, fr_ok = sem("f_done"), sem("fr_ok")
        srs_ok, srT_done, mxl_ok, srm_done = sem("srs_ok"), sem("srT_done"), sem("mxl_ok"), sem("srm_done")
        spread_ok, st_done, arg_ok, pexp_ok = sem("spread_ok"), sem("st_done"), sem("arg_ok"), sem("pexp_ok")
        pden_done, pn_ok, hs_done, hsT_ok = sem("pden_done"), sem("pn_ok"), sem("hs_done"), sem("hsT_ok")
        wf_done, yn_ok, x2_ok = sem("wf_done"), sem("yn_ok"), sem("x2_ok")
        xn2_ok, x2t_done, xT_ok = sem("xn2_ok"), sem("x2t_done"), sem("xT_ok")
        lg_done, top_ok, ew_ok, hot_ok, rank_done = sem("lg_done"), sem("top_ok"), sem("ew_ok"), sem("hot_ok"), sem("rank_done")
        base_ok, dest_ok, gate_ok = sem("base_ok"), sem("dest_ok"), sem("gate_ok")
        zero_ok, filled = sem("zero_ok"), sem("filled")
        scattered = sem("scattered")
        w1_in = [[sem(f"w1_in{i}_{n}") for n in range(PIECES)] for i in range(2)]
        w2_in = [sem(f"w2_in{n}") for n in range(2)]
        bias_in = [sem(f"bias_in{i}") for i in range(2)]
        xg_in, xgt_done, xgT_ok = sem("xg_in"), sem("xgt_done"), sem("xgT_ok")
        up_done, silu_ok, hid_ok, down_done = sem("up_done"), sem("silu_ok"), sem("hid_ok"), sem("down_done")
        yT_ok, yt_done, yrow_ok, y_stored = sem("yT_ok"), sem("yt_done"), sem("yrow_ok"), sem("y_stored")
        got_in = [sem(f"got_in{t}") for t in range(T)]
        res_ok, stored = sem("res_ok"), sem("stored")

        passed = {e.engine: sem(f"passed_{n}") for n, e in (("pe", nc.tensor), ("pool", nc.gpsimd), ("dve", nc.vector))}

        block = es.enter_context(nc.Block())

        ACT_J = [j for j in range(J) if j not in (1, 4, 7, 12)]
        DVE_J = [1, 4, 7, 12]

        def hold(eng, sem_, value):
            eng.wait_ge(sem_, value)
            eng.sem_inc(passed[eng.engine], 1)

        def chunk_range(eng, e):
            lo = eng.value_load(base_i[0:1, bass.ds(e, 1)], min_val=0, max_val=CH_MAX - 1)
            hi = eng.value_load(base_i[0:1, bass.ds(e + 1, 1)], min_val=1, max_val=CH_MAX)
            return lo, hi

        @block.sync
        def _(sp):
            for t in range(T):
                sp.dma_start(xres[:, t, :], x[t * P:(t + 1) * P, :]).then_inc(x_in, 16)
            sp.dma_start(wq_s, wq).then_inc(wqk_in, 16)
            sp.dma_start(wk_s, wk).then_inc(wqk_in, 16)

            def load_ctx(b, r):
                rows = ctx_in[b, :, :] if isinstance(b, int) else ctx_in[bass.ds(b, 1), :, :].rearrange("o k d -> (o k) d")
                sp.dma_start(ctx[r][:, 0:JF, :],
                             rows[0:JF * P, :].rearrange("(p j) d -> p j d", j=JF)).then_inc(ctx_in_s[r], 16)
                sp.dma_start(ctx[r][0:REST, JF, :], rows[JF * P:KEYS, :]).then_inc(ctx_rest[r], 16)

            load_ctx(0, 0)
            load_ctx(1, 1)
            for src, dst in ((wv, wv_s), (wo, wo_s), (wl, wl_s), (wr, wr_s), (wf, wf_s)):
                sp.dma_start(dst, src).then_inc(wc_in, 16)
            with sp.Fori(1, B // 2) as i:
                for r in range(2):
                    sp.wait_ge(av_done, i * 2 + (r - 1))
                    load_ctx(i * 2 + r, r)

            def load_expert(e, r):
                sp.dma_start(b1_s[r].rearrange("p a m -> p (a m)"), b1[bass.ds(e, 1), :, :].rearrange("o p m -> (o p) m")).then_inc(bias_in[r], 16)
                sp.dma_start(b2_s[r], b2[bass.ds(e, 1), :, :].rearrange("o p m -> (o p) m")).then_inc(bias_in[r], 16)
                for n in range(PIECES):
                    sp.dma_start(w1buf[r][:, n * MP:(n + 1) * MP, :, :].rearrange("p m a k c -> p (m a k c)"),
                                 w1[bass.ds(e, 1), :, n * (NW1 // PIECES):(n + 1) * (NW1 // PIECES)].rearrange("o p c -> (o p) c"))\
                      .then_inc(w1_in[r][n], 16)

            def load_down(e):
                for n in range(2):
                    sp.dma_start(w2buf[:, n * (M2 // 2):(n + 1) * (M2 // 2), :].rearrange("p m d -> p (m d)"),
                                 w2[bass.ds(e, 1), :, n * (NW2 // 2):(n + 1) * (NW2 // 2)].rearrange("o p c -> (o p) c"))\
                      .then_inc(w2_in[n], 16)

            sp.wait_ge(av_done, B)
            sp.wait_ge(filled, 32 * ((CH_MAX + 2) * W // P))
            load_expert(0, 0)
            load_down(0)
            sp.wait_ge(lg_done, T)
            sp.wait_ge(pn_ok, T)
            load_expert(1, 1)
            sp.wait_ge(base_ok, 1)
            with sp.Fori(0, E // 2 - 1) as ep:
                for r in range(2):
                    _, hi = chunk_range(sp, ep * 2 + r)
                    sp.wait_ge(down_done, hi)
                    load_down(ep * 2 + (r + 1))
                    sp.wait_ge(yT_ok, hi + 1)
                    load_expert(ep * 2 + (r + 2), r)
            _, hi = chunk_range(sp, E - 2)
            sp.wait_ge(down_done, hi)
            load_down(E - 1)
            for t in range(T):
                sp.wait_ge(res_ok, 2 * (t + 1))
                sp.dma_start(out[t * P:(t + 1) * P, :], xres[:, t, :]).then_inc(stored, 16)
            sp.wait_ge(stored, 16 * T)

        @block.gpsimd
        def _(pool):
            g = nc.gpsimd
            o = Order(pool, p_order)
            o.link(g.memset(ident, 0.0))
            o.link(g.memset(ones, 1.0))
            o.link(g.memset(same, 0.0))
            o.link(g.memset(below, 1.0))
            o.link(g.memset(place, 0.0))
            o.link(g.memset(half, -0.5))
            o.link(g.memset(tri.rearrange("p a b -> p (a b)"), 0.0))
            for e in range(E):
                o.link(g.memset(iota[:, e:e + 1], float(e)))
            for n in range(7):
                o.link(g.memset(over[:, n:n + 1], float(W * (n + 1))))
            o.settle()
            o.link(g.affine_select(out=ident, in_=ident, compare_op=ALU.not_equal, fill=1.0, base=0,
                                   pattern=[[-1, P]], channel_multiplier=1))
            o.link(g.affine_select(out=below, in_=below, compare_op=ALU.is_ge, fill=0.0, base=-1,
                                   pattern=[[1, P]], channel_multiplier=-1))
            o.link(g.affine_select(out=place, in_=place, compare_op=ALU.not_equal, fill=1.0, base=0,
                                   pattern=[[-1, S]], channel_multiplier=1))
            o.link(g.affine_select(out=place, in_=place, compare_op=ALU.not_equal, fill=1.0, base=-S,
                                   pattern=[[-1, S]], channel_multiplier=1))
            for i in range(2):
                o.link(g.memset(same[i * S:(i + 1) * S, i * S:(i + 1) * S], 1.0))
            for e in range(1, E + 1):
                o.link(g.memset(tri[:, e, 0:e], 1.0))
            o.link(g.memset(sc[64:P, JF, :], LOWEST))
            o.settle()
            g.memset(zeros, 0.0).then_inc(const_ok, 1)
            pool.wait_ge(const_ok, 1)
            for n in range((CH_MAX + 2) * W // P):
                pool.dma_start(rows_in[n * P:(n + 1) * P, :], zeros).then_inc(filled, 16)
                pool.dma_start(rows_out[n * P:(n + 1) * P, :], zeros).then_inc(filled, 16)

            def layer_rstd(n):
                pool.wait_ge(var_ok, n + 1)
                g.tensor_tensor(rstd[:, n % T:n % T + 1], mv[:, n % T, 1:2], half, ALU.pow).then_inc(rstd_ok, 1)

            for n in range(T):
                layer_rstd(n)
            pool.wait_ge(wide_in, 16)
            for t in range(T):
                pool.wait_ge(xn_ok, t + 1)
                g.tensor_tensor(xres[:, t, :], xres[:, t, :], bo_s, ALU.add).then_inc(xb_ok, 1)
            for n in range(T, 3 * T):
                layer_rstd(n)
            for t in range(T):
                pool.wait_ge(yn_ok, t + 1)
                if t == 0:
                    pool.wait_ge(wide_in, 48)
                buf = xn[:, t, :]
                o.link(g.tensor_tensor(buf, buf, gamma_s, ALU.mult))
                o.link(g.tensor_tensor(buf, buf, beta_s, ALU.add))
                g.tensor_tensor(xres[:, t, :], xres[:, t, :], buf, ALU.add).then_inc(x2_ok, 1)
            for n in range(3 * T, 4 * T):
                layer_rstd(n)
            pool.wait_ge(filled, 32 * ((CH_MAX + 2) * W // P))
            pool.wait_ge(dest_ok, 1)
            pool.wait_ge(xn2_ok, T)
            for k in range(2):
                for t in range(T):
                    pool.indirect_dma_start(
                        out=rows_in, out_offset=bass.IndirectOffsetOnAxis(ap=dest_i[:, k, t:t + 1].bitcast(U32), axis=0),
                        in_=xn[:, t, :], in_offset=None).then_inc(scattered, 16)
            pool.wait_ge(gate_ok, 1)
            pool.wait_ge(scattered, 16 * 2 * T)
            g.memset(yT.rearrange("p a b -> p (a b)"), 0.0).then_inc(yT_ok, 1)
            g.memset(yrow, 0.0).then_inc(zero_ok, 1)
            pool.wait_ge(zero_ok, 1)
            pool.dma_start(rows_out[(CH_MAX + 1) * W:(CH_MAX + 2) * W, :], yrow).then_inc(y_stored, 16)
            pool.dma_start(xg, rows_in[0:W, :]).then_inc(xg_in, 16)

            pool.wait_ge(base_ok, 1)
            total = pool.value_load(base_i[0:1, E:E + 1], min_val=1, max_val=CH_MAX)
            with pool.Fori(0, total) as c:
                pool.wait_ge(xgt_done, c + 1)
                pool.dma_start(xg, rows_in[bass.ds(c * W + W, W), :]).then_inc(xg_in, 16)
                pool.wait_ge(yrow_ok, c + 1)
                pool.dma_start(rows_out[bass.ds(c * W, W), :], yrow).then_inc(y_stored, 16)
            pool.wait_ge(yrow_ok, total + 1)
            pool.dma_start(rows_out[bass.ds(total * W, W), :], yrow).then_inc(y_stored, 16)
            hold(pool, y_stored, (total + 2) * 16)
            hold(pool, down_done, total)
            for t in range(T):
                for k in range(2):
                    pool.indirect_dma_start(
                        out=got[:, k, t, :], out_offset=None, in_=rows_out,
                        in_offset=bass.IndirectOffsetOnAxis(ap=from_i[:, k, t:t + 1].bitcast(U32), axis=0)).then_inc(got_in[t], 16)

        @block.scalar
        def _(act):
            a = nc.scalar
            for dst, src in ((bq_s, bq), (bk_s, bk), (bv_s, bv)):
                act.dma_start(dst, src).then_inc(small_in, 16)
            act.dma_start(rw_s, rw).then_inc(small_in, 16)
            act.dma_start(bo_s, bo.partition_broadcast(P)).then_inc(wide_in, 16)
            act.dma_start(rb_s, rb.partition_broadcast(P)).then_inc(small_in, 16)
            act.dma_start(attl_s, att_l.partition_broadcast(P)).then_inc(small_in, 16)
            act.dma_start(attr_s, att_r.partition_broadcast(P)).then_inc(small_in, 16)
            for t in range(T):
                act.wait_ge(xt_done, t + 1)
                a.activation(xnT[:, :, t * P:(t + 1) * P], bank[2 + t][:, :].rearrange("p (k c) -> p k c", k=KD),
                             ACT.Copy).then_inc(xnT_ok, 1)
            act.wait_ge(small_in, 16 * 7)
            for m in range(KD):
                act.wait_ge(q_done, m + 1)
                a.activation(qT[:, m, :], bank[(0, 1, 6, 7)[m]][:, :], ACT.Identity,
                             bias=bq_s[:, m:m + 1]).then_inc(qT_ok, 1)
            for m in range(KD):
                act.wait_ge(qk_done, m + 1)
                a.activation(qkT[:, m, :], bank[2 + m][:, :], ACT.Copy).then_inc(qkT_ok, 1)
            act.wait_ge(bkq_done, 1)
            a.activation(bkq, bank[0][:, :], ACT.Copy).then_inc(bkq_ok, 1)

            def turned(b, j):
                act.wait_ge(turn_done, b * J + (j + 1))
                n = REST if j == JF else P
                a.activation(ctxT[j % NRING][:, :, 0:n],
                             bank[2 + j % 3][:, :].rearrange("p (k c) -> p k c", k=KD)[:, :, 0:n],
                             ACT.Copy).then_inc(turn_act, 1)

            def exps(b):
                act.wait_ge(sub_ok, b + 1)
                a.activation(pr.rearrange("p j q -> p (j q)"), pr.rearrange("p j q -> p (j q)"), ACT.Exp,
                             scale=SCALE).then_inc(exp_ok, 1)

            def batch(b, more=True):
                for j in ACT_J:
                    if more:
                        turned(b + 1, j)
                exps(b)

            for j in ACT_J:
                turned(0, j)
            with act.Fori(0, B - 1) as b:
                batch(b)
            batch(B - 1, more=False)

            act.wait_ge(aT_ok, B)
            act.dma_start(gamma_s, gamma.partition_broadcast(P)).then_inc(wide_in, 16)
            act.dma_start(beta_s, beta.partition_broadcast(P)).then_inc(wide_in, 16)
            for m in range(KD):
                act.wait_ge(v_done, m + 1)
                a.activation(vT[:, m, :], bank[m][:, :], ACT.Identity, bias=bv_s[:, m:m + 1]).then_inc(vT_ok, 1)
            for t in range(T):
                act.wait_ge(ht_done, t + 1)
                a.activation(hT[:, :, t * P:(t + 1) * P], bank[t][:, :].rearrange("p (k c) -> p k c", k=KD),
                             ACT.Copy).then_inc(hT_ok, 1)
            for t in range(T):
                act.wait_ge(f_done, 2 * t + 2)
                a.activation(fr[:, t, :], bank[t][:, :], ACT.Copy).then_inc(fr_ok, 1)
            for t in range(T):
                act.wait_ge(arg_ok, t + 1)
                a.activation(att_tmp[:, t, :], att_tmp[:, t, :], ACT.Exp).then_inc(pexp_ok, 1)
            for t in range(T):
                for b2_ in range(2):
                    act.wait_ge(hs_done, 2 * t + b2_ + 1)
                    a.activation(hsT[:, :, t * P + b2_ * S:t * P + (b2_ + 1) * S],
                                 bank[4 + 2 * (t % 2) + b2_][:, 0:KD * S].rearrange("p (k c) -> p k c", k=KD),
                                 ACT.Copy).then_inc(hsT_ok, 1)
            for t in range(T):
                act.wait_ge(x2t_done, t + 1)
                a.activation(xT[:, :, t * P:(t + 1) * P], bank[t][:, :].rearrange("p (k c) -> p k c", k=KD),
                             ACT.Copy).then_inc(xT_ok, 1)
            act.wait_ge(top_ok, 1)
            a.activation(ew, ew, ACT.Exp).then_inc(ew_ok, 1)

            act.wait_ge(base_ok, 1)
            with act.Fori(0, E // 2) as ep:
                for r in range(2):
                    lo, hi = chunk_range(act, ep * 2 + r)
                    act.wait_ge(bias_in[r], ep * 32 + 32)
                    with act.Fori(lo, hi) as c:
                        for m in range(M2):
                            act.wait_ge(up_done, c * M2 + (m + 1))
                            a.activation(act_s[m % 4], bank[m % 4][:, 0:W], ACT.Silu,
                                         bias=b1_s[r][:, 0, m:m + 1]).then_inc(silu_ok, 1)
                            if m == 3:
                                act.wait_ge(yt_done, c + 1)
                                act.wait_ge(y_stored, c * 16 + 16)
                                a.activation(yrow, bank[6][0:W, :], ACT.Copy).then_inc(yrow_ok, 1)
                        act.wait_ge(down_done, c + 1)
                        for k in range(KD):
                            ins = a.activation(yT[:, k, :], bank[4][:, k * W:(k + 1) * W], ACT.Identity,
                                               bias=b2_s[r][:, k:k + 1])
                        ins.then_inc(yT_ok, 1)
            total = act.value_load(base_i[0:1, E:E + 1], min_val=1, max_val=CH_MAX)
            act.wait_ge(yt_done, total + 1)
            act.wait_ge(y_stored, total * 16 + 16)
            a.activation(yrow, bank[6][0:W, :], ACT.Copy).then_inc(yrow_ok, 1)

        @block.tensor
        def _(pe):
            mm = nc.tensor.matmul

            def tr(dst, src, n=P):
                return nc.tensor.transpose(dst, src, ident[0:n, 0:n])

            def blocks(dst, lhs, rhs):
                for k in range(KD):
                    ins = mm(dst, lhs(k), rhs(k), start=(k == 0), stop=(k == KD - 1))
                return ins

            pe.wait_ge(const_ok, 1)
            for t in range(T):
                pe.wait_ge(xn_ok, t + 1)
                for k in range(KD):
                    ins = tr(bank[2 + t][:, k * P:(k + 1) * P], xn[:, t, k * P:(k + 1) * P])
                ins.then_inc(xt_done, 1)
            pe.wait_ge(xnT_ok, T)
            pe.wait_ge(wqk_in, 32)
            for m in range(KD):
                blocks(bank[(0, 1, 6, 7)[m]][:, :], lambda k: wq_s[:, k, m * P:(m + 1) * P], lambda k: xnT[:, k, :])\
                    .then_inc(q_done, 1)
            pe.wait_ge(qT_ok, KD)
            for m in range(KD):
                blocks(bank[2 + m][:, :], lambda k: wk_s[:, k, m * P:(m + 1) * P], lambda k: qT[:, k, :])\
                    .then_inc(qk_done, 1)
            pe.wait_ge(bkw_ok, 1)
            blocks(bank[0][:, :], lambda k: bk_wide[:, k, :], lambda k: qT[:, k, :]).then_inc(bkq_done, 1)
            pe.wait_ge(qkT_ok, KD)
            pe.wait_ge(bkq_ok, 1)

            def turn(b, r, j):
                n = REST if j == JF else P
                for k in range(KD):
                    ins = tr(bank[2 + j % 3][:, k * P:k * P + n], ctx[r][0:n, j, k * P:(k + 1) * P], n)
                ins.then_inc(turn_done, 1)

            def scores(b, j):
                n = REST if j == JF else P
                if j in DVE_J:
                    pe.wait_ge(turn_dve, b * len(DVE_J) + (DVE_J.index(j) + 1))
                else:
                    pe.wait_ge(turn_act, b * len(ACT_J) + (ACT_J.index(j) + 1))
                ins = blocks(bank[j // 8][0:n, (j % 8) * S:(j % 8 + 1) * S],
                             lambda k: ctxT[j % NRING][:, k, 0:n], lambda k: qkT[:, k, bass.ds(b * S, S)])
                if j == J - 1:
                    ins.then_inc(sc_done, 1)

            def row_max(b):
                hold(pe, mx_ok, b + 1)
                tr(bank[6][0:S, 0:P], mx).then_inc(mxT_done, 1)

            def spread_max(b):
                pe.wait_ge(dg_ok, b + 1)
                mm(bank[6][:, P:P + S], ones[0:S, :], dg[0:S, :], start=True, stop=True).then_inc(mxb_done, 1)

            def all_scores(b, r, between):
                for n in range(J + 2):
                    if n < J:
                        if n == 0:
                            pe.wait_ge(ctx_in_s[r], (b // 2 + 1) * 16 if isinstance(b, int) else ctx_count(b, r))
                        if n == JF:
                            pe.wait_ge(ctx_rest[r], (b // 2 + 1) * 16 if isinstance(b, int) else ctx_count(b, r))
                        turn(b, r, n)
                    if n >= 2:
                        scores(b, n - 2)
                    for at_, f in between:
                        if n == at_:
                            f()

            def ctx_count(b, r):
                return (b - r) * 8 + 16

            def weigh(b, r):
                pe.wait_ge(exp_ok, b + 1)
                for k in range(KD):
                    for j in range(J):
                        n = REST if j == JF else P
                        ins = mm(bank[5][:, k * S:(k + 1) * S], ctx[r][0:n, j, k * P:(k + 1) * P], pr[0:n, j, :],
                                 start=(j == 0), stop=(j == J - 1))
                    if k == 1:
                        pe.wait_ge(dsum_ok, b + 1)
                        mm(bank[7][:, 0:S], ones, dsum, start=True, stop=True).then_inc(den_done, 1)
                ins.then_inc(av_done, 1)

            all_scores(0, 0, [])
            def step(b, r):
                pe.wait_ge(sc_out, b + 1)
                all_scores(b + 1, 1 - r, [(5, lambda: row_max(b)), (9, lambda: spread_max(b))])
                weigh(b, r)
                pe.wait_ge(aT_ok, b + 1)

            with pe.Fori(0, B // 2 - 1) as i:
                step(i * 2, 0)
                step(i * 2 + 1, 1)
            step(B - 2, 0)
            pe.wait_ge(sc_out, B)
            row_max(B - 1)
            spread_max(B - 1)
            weigh(B - 1, 1)

            pe.wait_ge(aT_ok, B)
            pe.wait_ge(wc_in, 16 * 5)
            for m in range(KD):
                blocks(bank[m][:, :], lambda k: wv_s[:, k, m * P:(m + 1) * P], lambda k: aT[:, k, :]).then_inc(v_done, 1)
            pe.wait_ge(vT_ok, KD)
            for t in range(T):
                blocks(bank[4 + t][:, :], lambda k: vT[:, k, t * P:(t + 1) * P], lambda k: wo_s[:, k, :]).then_inc(o_done, 1)
            for t in range(T):
                pe.wait_ge(h_ok, t + 1)
                for k in range(KD):
                    ins = tr(bank[t][:, k * P:(k + 1) * P], h_nat[:, t, k * P:(k + 1) * P])
                ins.then_inc(ht_done, 1)
            for t in range(T):
                pe.wait_ge(hT_ok, t + 1)
                blocks(bank[4 + t][:, :], lambda k: hT[:, k, t * P:(t + 1) * P], lambda k: wl_s[:, k, :]).then_inc(f_done, 1)
                blocks(bank[t][:, :], lambda k: hT[:, k, t * P:(t + 1) * P], lambda k: wr_s[:, k, :]).then_inc(f_done, 1)
            for t in range(T):
                pe.wait_ge(srs_ok, t + 1)
                tr(bank[4 + t][0:H, 0:P], sr[:, t, :]).then_inc(srT_done, 1)
                pe.wait_ge(mxl_ok, t + 1)
                mm(bank[4 + t][:, 256:256 + H], mxl[0:H, :], ident[0:H, 0:H], start=True, stop=True).then_inc(srm_done, 1)
            def self_scores(t):
                pe.wait_ge(spread_ok, t + 1)
                if t == 0:
                    pe.wait_ge(fr_ok, T)
                mm(bank[0][:, :], same, spread[:, 0, :, :].rearrange("p h n -> p (h n)"), start=True, stop=True)
                mm(bank[1][:, :], same, spread[:, 1, :, :].rearrange("p h n -> p (h n)"), start=True, stop=True).then_inc(st_done, 1)

            def self_weigh(t):
                pe.wait_ge(pexp_ok, t + 1)
                mm(bank[2 + t % 2][:, :], same, att_tmp[:, t, :], start=True, stop=True).then_inc(pden_done, 1)
                pe.wait_ge(pn_ok, t + 1)
                if t >= 2:
                    pe.wait_ge(hsT_ok, 2 * (t - 1))
                for b_ in range(2):
                    for h in range(H):
                        q = (h % 2) * HD
                        ins = mm(bank[4 + 2 * (t % 2) + b_][q:q + HD, (h // 2) * S:(h // 2 + 1) * S],
                                 fr[b_ * S:(b_ + 1) * S, t, h * HD:(h + 1) * HD],
                                 att_tmp[b_ * S:(b_ + 1) * S, t, h * S:(h + 1) * S], start=True, stop=True)
                    ins.then_inc(hs_done, 1)

            self_scores(0)
            for t in range(T):
                if t + 1 < T:
                    self_scores(t + 1)
                self_weigh(t)
            for t in range(T):
                pe.wait_ge(hsT_ok, 2 * t + 2)
                blocks(bank[t][:, :], lambda k: hsT[:, k, t * P:(t + 1) * P], lambda k: wf_s[:, k, :]).then_inc(wf_done, 1)
            for t in range(T):
                pe.wait_ge(xn2_ok, t + 1)
                for k in range(KD):
                    ins = tr(bank[t][:, k * P:(k + 1) * P], xn[:, t, k * P:(k + 1) * P])
                ins.then_inc(x2t_done, 1)
            for t in range(T):
                pe.wait_ge(xT_ok, t + 1)
                blocks(bank[4][:, t * E:(t + 1) * E], lambda k: xT[:, k, t * P:(t + 1) * P], lambda k: rw_s[:, k, :])\
                    .then_inc(lg_done, 1)
            pe.wait_ge(hot_ok, 1)
            for t in range(T):
                mm(bank[5][:, t * E:(t + 1) * E], below, both[:, t, :], start=True, stop=(t == 0))
                for u in range(t):
                    mm(bank[5][:, t * E:(t + 1) * E], ones, both[:, u, :], start=False, stop=(u == t - 1))
            for t in range(T):
                ins = mm(bank[5][:, T * E:(T + 1) * E], ones, both[:, t, :], start=(t == 0), stop=(t == T - 1))
            ins.then_inc(rank_done, 1)

            def turn_rows(n):
                hold(pe, xg_in, n)
                for k in range(KD):
                    ins = tr(bank[5][:, k * W:(k + 1) * W], xg[:, k * P:(k + 1) * P], W)
                ins.then_inc(xgt_done, 1)

            def turn_results(n):
                hold(pe, yT_ok, n)
                for k in range(KD):
                    ins = tr(bank[6][0:W, k * P:(k + 1) * P], yT[:, k, :])
                ins.then_inc(yt_done, 1)

            def up(r, m):
                for a_ in range(2):
                    for k in range(KD):
                        ins = mm(bank[m % 4][:, a_ * W:(a_ + 1) * W], w1buf[r][:, m, a_, k, :], xgT[:, k, :],
                                 start=(k == 0), stop=(k == KD - 1))
                ins.then_inc(up_done, 1)

            def down(c, m):
                pe.wait_ge(hid_ok, c * M2 + (m + 1))
                for k in range(KD):
                    ins = mm(bank[4][:, k * W:(k + 1) * W], w2buf[:, m, k * P:(k + 1) * P], hid[:, m, :],
                             start=(m == 0 and k == 0), stop=(m == M2 - 1), skip_group_check=True)
                if m == M2 - 1:
                    ins.then_inc(down_done, 1)

            turn_rows(16)
            with pe.Fori(0, E // 2) as ep:
                for r in range(2):
                    lo, hi = chunk_range(pe, ep * 2 + r)
                    with pe.Fori(lo, hi) as c:
                        pe.wait_ge(xgT_ok, c + 1)
                        for m in range(M2):
                            if m % MP == 0:
                                pe.wait_ge(w1_in[r][m // MP], ep * 16 + 16)
                            up(r, m)
                            if m == 1:
                                turn_results(c + 1)
                            if m >= LAG:
                                if (m - LAG) % (M2 // 2) == 0:
                                    pe.wait_ge(w2_in[(m - LAG) // (M2 // 2)], ep * 32 + (16 * r + 16))
                                down(c, m - LAG)
                            if m == M2 - 2:
                                turn_rows(c * 16 + 32)
                        for m in range(M2 - LAG, M2):
                            down(c, m)
            total = pe.value_load(base_i[0:1, E:E + 1], min_val=1, max_val=CH_MAX)
            turn_results(total + 1)

        @block.vector
        def _(dve):
            v = nc.vector
            o = Order(dve, v_order)

            def norm_stats(n, src):
                t = n % T
                o.link(v.bn_stats(stats[:, t, :], src))
                o.link(v.bn_aggr(mv[:, t, :], stats[:, t, :]))
                v.tensor_scalar(mv[:, t, 1:2], mv[:, t, 1:2], EPS, None, ALU.add).then_inc(var_ok, 1)

            def normalise(n, dst, src):
                t = n % T
                dve.wait_ge(rstd_ok, n + 1)
                return v.tensor_scalar(dst, src, mv[:, t, 0:1], rstd[:, t:t + 1], ALU.subtract, ALU.mult)

            for t in range(T):
                if t == 0:
                    dve.wait_ge(x_in, 16 * T)
                norm_stats(t, xres[:, t, :])
            for t in range(T):
                normalise(t, xn[:, t, :], xres[:, t, :]).then_inc(xn_ok, 1)
            dve.wait_ge(small_in, 16 * 7)
            v.tensor_copy(bk_wide, bk_s.unsqueeze(2).to_broadcast([P, KD, P])).then_inc(bkw_ok, 1)

            def turned(b, j):
                dve.wait_ge(turn_done, b * J + (j + 1))
                n = REST if j == JF else P
                v.tensor_copy(ctxT[j % NRING][:, :, 0:n],
                              bank[2 + j % 3][:, :].rearrange("p (k c) -> p k c", k=KD)[:, :, 0:n]).then_inc(turn_dve, 1)

            def take_scores(b):
                ob = Order(dve, sc_order, b * 2)
                dve.wait_ge(sc_done, b + 1)
                bias = bkq[:, bass.ds(b * S, S)]
                b0 = bank[0][:, :].rearrange("p (j q) -> p j q", q=S)
                b1_ = bank[1][:, :].rearrange("p (j q) -> p j q", q=S)
                ob.step(v.tensor_tensor(sc[:, 0:8, :], b0, bias.unsqueeze(1).to_broadcast([P, 8, S]), ALU.add))
                ob.step(v.tensor_tensor(sc[:, 8:JF, :], b1_[:, 0:JF - 8, :],
                                        bias.unsqueeze(1).to_broadcast([P, JF - 8, S]), ALU.add))
                v.tensor_tensor(sc[0:REST, JF, :], b1_[0:REST, JF - 8, :],
                                bias[0:REST, :], ALU.add).then_inc(sc_out, 1)
                ob.settle()
                dve.wait_ge(sc_out, b + 1)
                v.tensor_reduce(mx, sc.rearrange("p j q -> p q j"), AX.X, ALU.max).then_inc(mx_ok, 1)

            def batch_max(b):
                ob = Order(dve, mxr_ok, b)
                dve.wait_ge(mxT_done, b + 1)
                ob.link(v.tensor_reduce(mxr[0:S, :], bank[6][0:S, 0:P], AX.X, ALU.max))
                v.tensor_scalar(dg[0:S, :], ident[0:S, 0:S], mxr[0:S, 0:1], None, ALU.mult).then_inc(dg_ok, 1)

            def less_max(b):
                dve.wait_ge(mxb_done, b + 1)
                v.tensor_tensor(pr, sc, bank[6][:, P:P + S].unsqueeze(1).to_broadcast([P, J, S]),
                                ALU.subtract).then_inc(sub_ok, 1)

            def sum_exps(b):
                dve.wait_ge(exp_ok, b + 1)
                v.tensor_reduce(dsum, pr.rearrange("p j q -> p q j"), AX.X, ALU.add).then_inc(dsum_ok, 1)

            def attended(b):
                ob = Order(dve, rec_ok, b)
                dve.wait_ge(den_done, b + 1)
                ob.link(v.reciprocal(rec, bank[7][:, 0:S]))
                dve.wait_ge(av_done, b + 1)
                v.tensor_tensor(aT[:, :, bass.ds(b * S, S)], bank[5][:, 0:KD * S].rearrange("p (k q) -> p k q", k=KD),
                                rec.unsqueeze(1).to_broadcast([P, KD, S]), ALU.mult).then_inc(aT_ok, 1)

            for j in DVE_J:
                turned(0, j)
            dve.wait_ge(bkq_ok, 1)
            take_scores(0)
            with dve.Fori(0, B - 1) as b:
                turned(b + 1, 1)
                turned(b + 1, 4)
                batch_max(b)
                turned(b + 1, 7)
                less_max(b)
                turned(b + 1, 12)
                sum_exps(b)
                take_scores(b + 1)
                attended(b)
            batch_max(B - 1)
            less_max(B - 1)
            sum_exps(B - 1)
            attended(B - 1)

            for t in range(T):
                dve.wait_ge(o_done, t + 1)
                dve.wait_ge(xb_ok, t + 1)
                o.link(v.tensor_tensor(xres[:, t, :], bank[4 + t][:, :], xres[:, t, :], ALU.add))
                norm_stats(T + t, xres[:, t, :])
                normalise(T + t, xn[:, t, :], xres[:, t, :]).then_inc(h_ok, 1)
            for t in range(T):
                for side, (att, dst) in enumerate(((attl_s, sl), (attr_s, sr))):
                    tmp = lk[side]
                    if side:
                        dve.wait_ge(fr_ok, t + 1)
                        o.link(v.scalar_tensor_tensor(out=tmp, in0=fr[:, t, :], scalar=0.01, in1=fr[:, t, :],
                                                      op0=ALU.mult, op1=ALU.max))
                    else:
                        dve.wait_ge(f_done, 2 * t + 1)
                        o.link(v.tensor_scalar(tmp, bank[4 + t][:, :], 0.01, None, ALU.mult))
                        o.link(v.tensor_tensor(tmp, bank[4 + t][:, :], tmp, ALU.max))
                    th = tmp.rearrange("p (h d) -> p h d", h=H)
                    o.link(v.tensor_tensor(th, th, att.unsqueeze(1).to_broadcast([P, H, HD]), ALU.mult))
                    ins = v.tensor_reduce(dst[:, t, :], th, AX.X, ALU.add)
                    if side:
                        ins.then_inc(srs_ok, 1)
                    else:
                        o.step(ins)
            o.settle()
            for t in range(T):
                dve.wait_ge(srT_done, t + 1)
                o.link(v.tensor_reduce(srx[0:H, :], bank[4 + t][0:H, 0:P].rearrange("h (b m) -> h b m", b=2), AX.X, ALU.max))
                v.tensor_copy(mxl[0:H, :].rearrange("h (b m) -> h b m", b=2),
                              srx[0:H, :].unsqueeze(2).to_broadcast([H, 2, S])).then_inc(mxl_ok, 1)
                dve.wait_ge(srm_done, t + 1)
                o.link(v.tensor_tensor(slm[:, t, :], sl[:, t, :], bank[4 + t][:, 256:256 + H], ALU.add))

            def spread_left(t):
                if t:
                    dve.wait_ge(st_done, t)
                wide = place.unsqueeze(1).to_broadcast([P, H, S])
                o.link(v.tensor_tensor(spread[:, 0, :, :], sl[:, t, :].unsqueeze(2).to_broadcast([P, H, S]), wide, ALU.mult))
                v.tensor_tensor(spread[:, 1, :, :], slm[:, t, :].unsqueeze(2).to_broadcast([P, H, S]), wide, ALU.mult)\
                    .then_inc(spread_ok, 1)

            spread_left(0)
            for t in range(T):
                dve.wait_ge(st_done, t + 1)
                dst = att_tmp[:, t, :]
                o.link(v.tensor_tensor(dst.rearrange("p (h n) -> p h n", h=H),
                                       bank[0][:, :].rearrange("p (h n) -> p h n", h=H),
                                       sr[:, t, :].unsqueeze(2).to_broadcast([P, H, S]), ALU.add))
                v.tensor_tensor(dst, dst, bank[1][:, :], ALU.subtract).then_inc(arg_ok, 1)
                if t + 1 < T:
                    dve.wait_ge(arg_ok, t + 1)
                    spread_left(t + 1)
                dve.wait_ge(pden_done, t + 1)
                o.link(v.reciprocal(lk[t % 2], bank[2 + t % 2][:, :]))
                v.tensor_tensor(dst, dst, lk[t % 2], ALU.mult).then_inc(pn_ok, 1)
            for t in range(T):
                dve.wait_ge(wf_done, t + 1)
                o.link(v.tensor_tensor(xn[:, t, :], bank[t][:, :], xn[:, t, :], ALU.add))
                norm_stats(2 * T + t, xn[:, t, :])
                normalise(2 * T + t, xn[:, t, :], xn[:, t, :]).then_inc(yn_ok, 1)
            for t in range(T):
                dve.wait_ge(x2_ok, t + 1)
                norm_stats(3 * T + t, xres[:, t, :])
                normalise(3 * T + t, xn[:, t, :], xres[:, t, :]).then_inc(xn2_ok, 1)

            dve.wait_ge(lg_done, T)
            wideE = lambda ap: ap.unsqueeze(2).to_broadcast([P, T, E])
            wideT = lambda ap: ap.unsqueeze(1).to_broadcast([P, T, E])
            o.link(v.tensor_tensor(lg, bank[4][:, 0:T * E].rearrange("p (t e) -> p t e", t=T), wideT(rb_s), ALU.add))

            def pick(src, best, hot):
                o.link(v.tensor_reduce(best, src, AX.X, ALU.max))
                o.link(v.tensor_tensor(eq, src, wideE(best), ALU.is_equal))
                o.link(v.tensor_scalar(eq, eq, -2.0 * E, 2.0 * E, ALU.mult, ALU.add))
                o.link(v.tensor_tensor(cand, eq, wideT(iota), ALU.add))
                o.link(v.tensor_reduce(idx, cand, AX.X, ALU.min))
                o.link(v.tensor_tensor(hot, wideT(iota), wideE(idx), ALU.is_equal))

            pick(lg, top[:, 0, :], oh1)
            o.link(v.tensor_scalar(lg2, oh1, LOWEST, None, ALU.mult))
            o.link(v.tensor_tensor(lg2, lg2, lg, ALU.add))
            pick(lg2, top[:, 1, :], oh2)
            v.tensor_tensor(both, oh1, oh2, ALU.add).then_inc(hot_ok, 1)
            v.tensor_tensor(ew, top[:, 1, :], top[:, 0, :], ALU.subtract).then_inc(top_ok, 1)
            dve.wait_ge(rank_done, 1)
            o.link(v.tensor_copy(cnt, bank[5][:, T * E:(T + 1) * E]))
            o.link(v.tensor_tensor(cmp7, cnt.unsqueeze(2).to_broadcast([P, E, 7]),
                                   over.unsqueeze(1).to_broadcast([P, E, 7]), ALU.is_gt))
            o.link(v.tensor_reduce(chs, cmp7, AX.X, ALU.add))
            o.link(v.tensor_scalar(chs, chs, 1.0, None, ALU.add))
            o.link(v.tensor_tensor(cmp9, chs.unsqueeze(1).to_broadcast([P, E + 1, E]), tri, ALU.mult))
            o.link(v.tensor_reduce(basef, cmp9, AX.X, ALU.add))
            v.tensor_copy(base_i[:, :], basef).then_inc(base_ok, 1)
            o.link(v.tensor_scalar(chs, basef[:, 0:E], float(W), None, ALU.mult))
            o.link(v.tensor_tensor(rank, bank[5][:, 0:T * E].rearrange("p (t e) -> p t e", t=T), wideT(chs), ALU.add))
            for k, hot in enumerate((oh1, oh2)):
                o.link(v.tensor_tensor(cand, hot, rank, ALU.mult))
                o.link(v.tensor_reduce(dst_f[:, k, :], cand, AX.X, ALU.add))
            o.link(v.tensor_copy(dest_i[:, :, :], dst_f))
            v.tensor_scalar(from_i[:, :, :], dst_f, float(W), None, ALU.add).then_inc(dest_ok, 1)
            dve.wait_ge(ew_ok, 1)
            o.link(v.tensor_scalar(wsum, ew, 1.0, None, ALU.add))
            o.link(v.reciprocal(gate[:, 0, :], wsum))
            v.tensor_tensor(gate[:, 1, :], gate[:, 0, :], ew, ALU.mult).then_inc(gate_ok, 1)

            dve.wait_ge(xgt_done, 1)
            dve.wait_ge(dest_ok, 1)
            dve.wait_ge(gate_ok, 1)
            v.tensor_copy(xgT, bank[5][:, 0:KD * W].rearrange("p (k c) -> p k c", k=KD)).then_inc(xgT_ok, 1)
            with dve.Fori(0, E // 2) as ep:
                for r in range(2):
                    lo, hi = chunk_range(dve, ep * 2 + r)
                    hold(dve, bias_in[r], ep * 32 + 32)
                    with dve.Fori(lo, hi) as c:
                        for m in range(M2):
                            if m == M2 - 1:
                                dve.wait_ge(xgt_done, c + 2)
                                dve.wait_ge(up_done, c * M2 + M2)
                                v.tensor_copy(xgT, bank[5][:, 0:KD * W].rearrange("p (k c) -> p k c", k=KD)).then_inc(xgT_ok, 1)
                            dve.wait_ge(silu_ok, c * M2 + (m + 1))
                            v.scalar_tensor_tensor(out=hid[:, m, :], in0=bank[m % 4][:, W:2 * W],
                                                   scalar=b1_s[r][:, 1, m:m + 1], in1=act_s[m % 4],
                                                   op0=ALU.add, op1=ALU.mult).then_inc(hid_ok, 1)
            for t in range(T):
                dve.wait_ge(got_in[t], 32)
                for k in range(2):
                    v.scalar_tensor_tensor(out=xres[:, t, :], in0=got[:, k, t, :], scalar=gate[:, k, t:t + 1],
                                           in1=xres[:, t, :], op0=ALU.mult, op1=ALU.add).then_inc(res_ok, 1)
                    if k == 0:
                        dve.wait_ge(res_ok, 2 * t + 1)


def kernel(**inputs):
    import numpy as np
    import concourse.bacc as bacc
    from concourse.bass_utils import run_bass_kernel_spmd

    a = {k: np.asarray(v) for k, v in inputs.items()}

    def cols(vec):
        return vec.reshape(-1, P).T

    def rows_of(mat):
        return mat.reshape(-1, P, mat.shape[1]).transpose(1, 0, 2)

    w1 = a["L0_ffn_w1"].reshape(E, 2, M2, P, KD, P)
    w2 = a["L0_ffn_w2"].reshape(E, D, M2, P)
    arrays = {
        "x": a["x"].reshape(TOK, D),
        "ctx": a["ctx_1024"],
        "wq": rows_of(a["L0_xattn_Wq"].T), "bq": cols(a["L0_xattn_bq"]),
        "wk": rows_of(a["L0_xattn_Wk"]), "bk": cols(a["L0_xattn_bk"]),
        "wv": rows_of(a["L0_xattn_Wv"].T), "bv": cols(a["L0_xattn_bv"]),
        "wo": rows_of(a["L0_xattn_Wo"].T), "bo": a["L0_xattn_bo"],
        "wl": rows_of(a["L0_attn_Wl"].T), "wr": rows_of(a["L0_attn_Wr"].T),
        "att_l": a["L0_attn_att_l"].reshape(HD), "att_r": a["L0_attn_att_r"].reshape(HD),
        "wf": rows_of(a["L0_attn_Wf"].T), "gamma": a["L0_attn_ln_gamma"], "beta": a["L0_attn_ln_beta"],
        "rw": rows_of(a["L0_ffn_router_w"].T), "rb": a["L0_ffn_router_b"],
        "w1": w1.transpose(0, 5, 2, 1, 4, 3).reshape(E, P, M2 * 2 * KD * P),
        "b1": a["L0_ffn_b1"].reshape(E, 2, M2, P).transpose(0, 3, 1, 2).reshape(E, P, 2 * M2),
        "w2": w2.transpose(0, 3, 2, 1).reshape(E, P, M2 * D),
        "b2": a["L0_ffn_b2"].reshape(E, KD, P).transpose(0, 2, 1),
    }
    nc = bacc.Bacc("TRN2", target_bir_lowering=False, num_devices=1)
    ins, args = {}, []
    for name, arr in arrays.items():
        arr = np.ascontiguousarray(arr)
        ins[f"in_{name}"] = arr
        args.append(nc.dram_tensor(f"in_{name}", arr.shape, mybir.dt.from_np(arr.dtype), kind="ExternalInput").ap())
    args.append(nc.dram_tensor("out", (TOK, D), F32, kind="ExternalOutput").ap())
    perceiver_layer(nc, *args)
    r = run_bass_kernel_spmd(nc, [ins], core_ids=[0])
    return r.results[0]["out"].reshape(B, S, D)
```

```python
import concourse.bass as bass
from concourse import mybir
from contextlib import ExitStack

F32 = mybir.dt.float32
I32 = mybir.dt.int32
U32 = mybir.dt.uint32
ALU = mybir.AluOpType
ACT = mybir.ActivationFunctionType
AX = mybir.AxisListType

P = 128
B, S, D = 8, 64, 512
KEYS = 1601
TOK = B * S
T = TOK // P
KD = D // P
JF = KEYS // P
REST = KEYS - JF * P
J = JF + 1
H, HD = 8, 64
E, FF = 8, 2048
M2 = FF // P
W = 64
CH_MAX = 2 * TOK // W + E
PAIRS = B // 2
NC = (KEYS + 511) // 512
NCOLS = [min(512, KEYS - n * 512) for n in range(NC)]
PIECES = 4
SCALE = 1.0 / float(D / 16) ** 0.5
EPS = 1e-5
LOWEST = -3.0e38


class Order:

    def __init__(self, eng, sem, base=0):
        self.eng, self.sem, self.base, self.n = eng, sem, base, 0

    def step(self, ins):
        self.n += 1
        ins.then_inc(self.sem, 1)
        return self.n

    def settle(self, n=None):
        self.eng.wait_ge(self.sem, self.base + (self.n if n is None else n))

    def link(self, ins):
        self.step(ins)
        self.settle()


def perceiver_layer(nc, x, ctx_in, ctxT_in_, wq, bq, wk, bk, wv, bv, wo, bo, wl, wr, att_l, att_r, wf, gamma, beta,
                    rw, rb, w1, b1, w2, b2, out):
    es = ExitStack()

    def sem(name):
        return es.enter_context(nc.semaphore(name))

    with es:
        NW1 = M2 * 2 * KD * P
        NW2 = M2 * D
        NARENA = 53100
        arena = es.enter_context(nc.sbuf_tensor("arena", [P, NARENA], F32))
        psum = es.enter_context(nc.psum_tensor("psum", [P, 8 * 512], F32))
        bank = [psum[:, i * 512:(i + 1) * 512] for i in range(8)]
        base_i = es.enter_context(nc.sbuf_tensor("base_i", [P, E + 1], I32))
        dest_i = es.enter_context(nc.sbuf_tensor("dest_i", [P, 2, T], I32))
        rows_in = nc.dram_tensor("rows_in", [(CH_MAX + 2) * W, D], F32, kind="Internal").ap()
        rows_out = nc.dram_tensor("rows_out", [(CH_MAX + 2) * W, D], F32, kind="Internal").ap()

        def area(start, *shape):
            n = 1
            for s in shape:
                n *= s
            assert start + n <= NARENA
            v = arena[:, start:start + n]
            if len(shape) == 1:
                return v
            names = "abcd"[:len(shape)]
            return v.rearrange(f"p ({' '.join(names)}) -> p {' '.join(names)}",
                               **dict(zip(names[1:], shape[1:])))

        W1A, W2A, W1B = 0, NW1, NW1 + NW2
        w1buf = [area(W1A, PIECES, 2, KD, 512), area(W1B, PIECES, 2, KD, 512)]
        w2buf = area(W2A, M2, D)
        NT = 2 * KD * KEYS
        NCTX = J * D
        ctxT = [area(n * 2 * KD * 512, 2, KD, NCOLS[n]) for n in range(NC)]
        ctx = [area(NT + i * NCTX, J, D) for i in range(2)]
        at = NT
        wq_s = area(at, KD, D)
        wk_s = area(at + KD * D, KD, D)
        xnT = area(at + 2 * KD * D, KD, TOK)
        qT = area(at + 3 * KD * D, KD, TOK)
        NB = KD * D
        att_tmp = area(W1B, 4, 512)
        assert NT + 2 * NCTX <= W1B + 2048
        at = W1B + 2048
        wv_s, wo_s, wl_s, wr_s, wf_s = (area(at + i * NB, KD, D) for i in range(5))
        aT = area(at + 5 * NB, KD, TOK)
        qkT = area(at + 6 * NB, KD, TOK)
        vT = qkT
        hT = aT
        fr = wv_s.rearrange("p k d -> p (k d)").rearrange("p (t d) -> p t d", t=T)
        hsT = vT
        xT = hT
        assert 7 * NB + 2048 <= NW1
        at = W1B + NW1
        def take(*shape):
            nonlocal at
            v = area(at, *shape)
            n = 1
            for s in shape:
                n *= s
            at += n
            return v
        xres = take(T, D)
        xn = take(T, D)
        h_nat = xn
        ident = take(P)
        ones = take(P)
        same = take(P)
        below = take(P)
        place = take(S)
        bq_s, bk_s, bv_s = take(KD), take(KD), take(KD)
        iota = take(E)
        over = take(7)
        tri = take(E + 1, E)
        rb_s = take(E)
        rw_s = take(KD, E)
        attl_s, attr_s = take(HD), take(HD)
        stats, mv, rstd = take(T, 6), take(T, 2), take(T)
        half = take(1)
        gate = take(2, T)
        shared = at
        pr = take(KEYS)
        prT = take(J, P)
        qp = take(KD, P)
        ao = take(D)
        bkq = take(T)
        bkq1, mx, mxr, nb, den, rec = (take(1) for _ in range(6))
        bo_s = take(D)
        zeros = take(D)
        endB = at
        at = shared
        lk = [take(D) for _ in range(2)]
        spread = [take(2, H, S) for _ in range(1)][0]
        gamma_s, beta_s = take(D), take(D)
        sl, sr, slm, srx = take(T, H), take(T, H), take(T, H), take(2)
        mxl = take(P)
        lg, eq, cand, oh1, oh2, lg2, both, rank = (take(T, E) for _ in range(8))
        top = take(2, T)
        idx, ew, wsum = take(T), take(T), take(T)
        dst_f = take(2, T)
        cnt, chs, basef = take(E), take(E), take(E + 1)
        cmp7, cmp9 = take(E, 7), take(E + 1, E)
        endC = at
        at = shared
        b1_s = [take(PIECES, 512) for _ in range(2)]
        cols = take(D)
        b2_s = [cols[0:W, :], take(D)[0:W, :]]
        yrow = cols[W:P, :]
        xg = take(D)[0:W, :]
        xgT = take(KD, W)
        glu = [xn[:, 2, :], take(512)]
        hid = [xn[:, 3, :], take(512)]
        hidT = xn[:, 0:2, :].rearrange("p u (c n) -> p u c n", c=4)
        endD = at
        print("SBUF floats", endB, endC, endD)
        assert max(endB, endC, endD) <= NARENA, (endB, endC, endD)
        got = area(W1A, 2, T, D)

        x_in = sem("x_in")
        wqk_in = sem("wqk_in")
        small_in = sem("small_in")
        wide_in = sem("wide_in")
        ctxT_in = [sem(f"ctxT_in{n}") for n in range(NC)]
        ctx_in_s = sem("ctx_in")
        wc_in = sem("wc_in")
        const_ok = sem("const_ok")
        p_order, v_order, a_order = sem("p_order"), sem("v_order"), sem("a_order")
        rstd_ok = sem("rstd_ok")
        var_ok = sem("var_ok")
        xn_ok = sem("xn_ok")
        xb_ok = sem("xb_ok")
        xt_done, xnT_ok = sem("xt_done"), sem("xnT_ok")
        q_done, qT_ok = sem("q_done"), sem("qT_ok")
        qk_done, qkT_ok = sem("qk_done"), sem("qkT_ok")
        bkq_done, bkq_ok = sem("bkq_done"), sem("bkq_ok")
        qp_ok, sc_done, row_order, nb_ok, exp_ok = sem("qp_ok"), sem("sc_done"), sem("row_order"), sem("nb_ok"), sem("exp_ok")
        prt_done, prt_act, prt_dve = sem("prt_done"), sem("prt_act"), sem("prt_dve")
        av_done, rec_ok, ao_ok, at_done, aT_ok = sem("av_done"), sem("rec_ok"), sem("ao_ok"), sem("at_done"), sem("aT_ok")
        v_done, vT_ok = sem("v_done"), sem("vT_ok")
        o_done, x1_ok = sem("o_done"), sem("x1_ok")
        h_ok, ht_done, hT_ok = sem("h_ok"), sem("ht_done"), sem("hT_ok")
        f_done, fr_ok = sem("f_done"), sem("fr_ok")
        srs_ok, srT_done, mxl_ok, srm_done = sem("srs_ok"), sem("srT_done"), sem("mxl_ok"), sem("srm_done")
        spread_ok, st_done, arg_ok, pexp_ok = sem("spread_ok"), sem("st_done"), sem("arg_ok"), sem("pexp_ok")
        pden_done, pn_ok, hs_done, hsT_ok = sem("pden_done"), sem("pn_ok"), sem("hs_done"), sem("hsT_ok")
        wf_done, yn_ok, x2_ok = sem("wf_done"), sem("yn_ok"), sem("x2_ok")
        xn2_ok, x2t_done, xT_ok = sem("xn2_ok"), sem("x2t_done"), sem("xT_ok")
        lg_done, top_ok, ew_ok, hot_ok, rank_done = sem("lg_done"), sem("top_ok"), sem("ew_ok"), sem("hot_ok"), sem("rank_done")
        base_ok, dest_ok, gate_ok = sem("base_ok"), sem("dest_ok"), sem("gate_ok")
        zero_ok, filled = sem("zero_ok"), sem("filled")
        scattered = sem("scattered")
        w1_in = [[sem(f"w1_in{i}_{n}") for n in range(PIECES)] for i in range(2)]
        w2_in = [sem(f"w2_in{n}") for n in range(2)]
        bias_in = [sem(f"bias_in{i}") for i in range(2)]
        xg_in, xgt_done, xgT_ok = sem("xg_in"), sem("xgt_done"), sem("xgT_ok")
        up_done, lin_ok, silu_ok, hid_ok = sem("up_done"), sem("lin_ok"), sem("silu_ok"), sem("hid_ok")
        hidt_done, hidT_ok, down_done = sem("hidt_done"), sem("hidT_ok"), sem("down_done")
        sum_order, yrow_ok, y_stored = sem("sum_order"), sem("yrow_ok"), sem("y_stored")
        got_in = [sem(f"got_in{t}") for t in range(T)]
        res_ok, stored = sem("res_ok"), sem("stored")

        passed = {e.engine: sem(f"passed_{n}") for n, e in (("pe", nc.tensor), ("pool", nc.gpsimd), ("dve", nc.vector))}

        block = es.enter_context(nc.Block())

        def hold(eng, sem_, value):
            eng.wait_ge(sem_, value)
            eng.sem_inc(passed[eng.engine], 1)

        def chunk_range(eng, e):
            lo = eng.value_load(base_i[0:1, bass.ds(e, 1)], min_val=0, max_val=CH_MAX - 1)
            hi = eng.value_load(base_i[0:1, bass.ds(e + 1, 1)], min_val=1, max_val=CH_MAX)
            return lo, hi

        @block.sync
        def _(sp):
            for t in range(T):
                sp.dma_start(xres[:, t, :], x[t * P:(t + 1) * P, :]).then_inc(x_in, 16)
            sp.dma_start(wq_s, wq).then_inc(wqk_in, 16)
            sp.dma_start(wk_s, wk).then_inc(wqk_in, 16)

            def load_turned(i, n):
                o_ = n * 2 * KD * 512
                w_ = 2 * KD * NCOLS[n]
                sp.dma_start(ctxT[n].rearrange("p a k c -> p (a k c)"),
                             ctxT_in_[bass.ds(i, 1), :, o_:o_ + w_].rearrange("o p c -> (o p) c")).then_inc(ctxT_in[n], 16)

            def load_rows(i):
                for a_ in range(2):
                    rows = ctx_in[bass.ds(i * 2 + a_, 1), :, :].rearrange("o k d -> (o k) d")
                    sp.dma_start(ctx[a_][:, 0:JF, :],
                                 rows[0:JF * P, :].rearrange("(p j) d -> p j d", j=JF)).then_inc(ctx_in_s, 16)
                    sp.dma_start(ctx[a_][0:REST, JF, :], rows[JF * P:KEYS, :]).then_inc(ctx_in_s, 16)

            for n in range(NC):
                load_turned(0, n)
            sp.wait_ge(bkq_done, 1)
            load_rows(0)
            for src, dst in ((wv, wv_s), (wo, wo_s), (wl, wl_s), (wr, wr_s), (wf, wf_s)):
                sp.dma_start(dst, src).then_inc(wc_in, 16)
            with sp.Fori(1, PAIRS) as i:
                for n in range(NC):
                    sp.wait_ge(sc_done, i * NC + (n + 1 - NC))
                    load_turned(i, n)
                sp.wait_ge(av_done, i)
                load_rows(i)

            def load_biases(e, r):
                for a_ in range(2):
                    sp.dma_start(b1_s[r][a_ * W:(a_ + 1) * W, :, :].rearrange("p q c -> p (q c)"),
                                 b1[bass.ds(e, 1), a_, :].rearrange("o c -> (o c)").partition_broadcast(W)).then_inc(bias_in[r], 16)
                sp.dma_start(b2_s[r], b2[bass.ds(e, 1), :].rearrange("o c -> (o c)").partition_broadcast(W)).then_inc(bias_in[r], 16)

            def load_weights(e, r):
                for n in range(PIECES):
                    sp.dma_start(w1buf[r][:, n, :, :, :].rearrange("p a k c -> p (a k c)"),
                                 w1[bass.ds(e, 1), :, n * (NW1 // PIECES):(n + 1) * (NW1 // PIECES)].rearrange("o p c -> (o p) c"))\
                      .then_inc(w1_in[r][n], 16)

            def load_down(e):
                for n in range(2):
                    sp.dma_start(w2buf[:, n * (M2 // 2):(n + 1) * (M2 // 2), :].rearrange("p m d -> p (m d)"),
                                 w2[bass.ds(e, 1), :, n * (NW2 // 2):(n + 1) * (NW2 // 2)].rearrange("o p c -> (o p) c"))\
                      .then_inc(w2_in[n], 16)

            sp.wait_ge(av_done, PAIRS)
            load_weights(0, 0)
            load_down(0)
            sp.wait_ge(lg_done, T)
            sp.wait_ge(pn_ok, T)
            load_weights(1, 1)
            sp.wait_ge(gate_ok, 1)
            sp.wait_ge(scattered, 16 * 2 * T)
            load_biases(0, 0)
            load_biases(1, 1)
            sp.wait_ge(base_ok, 1)
            with sp.Fori(0, E // 2 - 1) as ep:
                for r in range(2):
                    _, hi = chunk_range(sp, ep * 2 + r)
                    sp.wait_ge(down_done, hi)
                    load_down(ep * 2 + (r + 1))
                    sp.wait_ge(yrow_ok, hi)
                    load_biases(ep * 2 + (r + 2), r)
                    load_weights(ep * 2 + (r + 2), r)
            _, hi = chunk_range(sp, E - 2)
            sp.wait_ge(down_done, hi)
            load_down(E - 1)
            for t in range(T):
                sp.wait_ge(res_ok, 2 * (t + 1))
                sp.dma_start(out[t * P:(t + 1) * P, :], xres[:, t, :]).then_inc(stored, 16)
            sp.wait_ge(stored, 16 * T)

        @block.gpsimd
        def _(pool):
            g = nc.gpsimd
            o = Order(pool, p_order)
            o.link(g.memset(ident, 0.0))
            o.link(g.memset(ones, 1.0))
            o.link(g.memset(same, 0.0))
            o.link(g.memset(below, 1.0))
            o.link(g.memset(place, 0.0))
            o.link(g.memset(half, -0.5))
            o.link(g.memset(tri.rearrange("p a b -> p (a b)"), 0.0))
            for e in range(E):
                o.link(g.memset(iota[:, e:e + 1], float(e)))
            for n in range(7):
                o.link(g.memset(over[:, n:n + 1], float(W * (n + 1))))
            o.settle()
            o.link(g.affine_select(out=ident, in_=ident, compare_op=ALU.not_equal, fill=1.0, base=0,
                                   pattern=[[-1, P]], channel_multiplier=1))
            o.link(g.affine_select(out=below, in_=below, compare_op=ALU.is_ge, fill=0.0, base=-1,
                                   pattern=[[1, P]], channel_multiplier=-1))
            o.link(g.affine_select(out=place, in_=place, compare_op=ALU.not_equal, fill=1.0, base=0,
                                   pattern=[[-1, S]], channel_multiplier=1))
            o.link(g.affine_select(out=place, in_=place, compare_op=ALU.not_equal, fill=1.0, base=-S,
                                   pattern=[[-1, S]], channel_multiplier=1))
            for i in range(2):
                o.link(g.memset(same[i * S:(i + 1) * S, i * S:(i + 1) * S], 1.0))
            for e in range(1, E + 1):
                o.link(g.memset(tri[:, e, 0:e], 1.0))
            o.settle()
            g.memset(zeros, 0.0).then_inc(const_ok, 1)
            pool.wait_ge(const_ok, 1)
            for n in range((CH_MAX + 2) * W // P):
                pool.dma_start(rows_in[n * P:(n + 1) * P, :], zeros).then_inc(filled, 16)
                pool.dma_start(rows_out[n * P:(n + 1) * P, :], zeros).then_inc(filled, 16)

            def layer_rstd(n):
                pool.wait_ge(var_ok, n + 1)
                g.tensor_tensor(rstd[:, n % T:n % T + 1], mv[:, n % T, 1:2], half, ALU.pow).then_inc(rstd_ok, 1)

            for n in range(T):
                layer_rstd(n)
            pool.wait_ge(wide_in, 16)
            for t in range(T):
                pool.wait_ge(xn_ok, t + 1)
                g.tensor_tensor(xres[:, t, :], xres[:, t, :], bo_s, ALU.add).then_inc(xb_ok, 1)
            def queries(i):
                g.tensor_copy(qp, qkT[:, :, bass.ds(i * P, P)]).then_inc(qp_ok, 1)

            pool.wait_ge(qkT_ok, KD)
            queries(0)
            with pool.Fori(1, PAIRS) as i:
                pool.wait_ge(sc_done, i * NC)
                queries(i)
            for n in range(T, 3 * T):
                layer_rstd(n)
            for t in range(T):
                pool.wait_ge(yn_ok, t + 1)
                if t == 0:
                    pool.wait_ge(wide_in, 48)
                buf = xn[:, t, :]
                o.link(g.tensor_tensor(buf, buf, gamma_s, ALU.mult))
                o.link(g.tensor_tensor(buf, buf, beta_s, ALU.add))
                g.tensor_tensor(xres[:, t, :], xres[:, t, :], buf, ALU.add).then_inc(x2_ok, 1)
            for n in range(3 * T, 4 * T):
                layer_rstd(n)
            pool.wait_ge(filled, 32 * ((CH_MAX + 2) * W // P))
            pool.wait_ge(dest_ok, 1)
            pool.wait_ge(xn2_ok, T)
            for k in range(2):
                for t in range(T):
                    pool.indirect_dma_start(
                        out=rows_in, out_offset=bass.IndirectOffsetOnAxis(ap=dest_i[:, k, t:t + 1].bitcast(U32), axis=0),
                        in_=xn[:, t, :], in_offset=None).then_inc(scattered, 16)
            pool.wait_ge(gate_ok, 1)
            pool.wait_ge(scattered, 16 * 2 * T)
            g.memset(yrow, 0.0).then_inc(zero_ok, 1)
            pool.wait_ge(zero_ok, 1)
            pool.dma_start(rows_out[(CH_MAX + 1) * W:(CH_MAX + 2) * W, :], yrow).then_inc(y_stored, 16)
            pool.dma_start(xg, rows_in[0:W, :]).then_inc(xg_in, 16)

            pool.wait_ge(base_ok, 1)
            total = pool.value_load(base_i[0:1, E:E + 1], min_val=1, max_val=CH_MAX)
            with pool.Fori(0, total) as c:
                pool.wait_ge(xgt_done, c + 1)
                pool.dma_start(xg, rows_in[bass.ds(c * W + W, W), :]).then_inc(xg_in, 16)
                pool.wait_ge(yrow_ok, c + 1)
                pool.dma_start(rows_out[bass.ds(c * W, W), :], yrow).then_inc(y_stored, 16)
            hold(pool, y_stored, (total + 1) * 16)
            for t in range(T):
                for k in range(2):
                    pool.indirect_dma_start(
                        out=got[:, k, t, :], out_offset=None, in_=rows_out,
                        in_offset=bass.IndirectOffsetOnAxis(ap=dest_i[:, k, t:t + 1].bitcast(U32), axis=0)).then_inc(got_in[t], 16)

        @block.scalar
        def _(act):
            a = nc.scalar
            for dst, src in ((bq_s, bq), (bk_s, bk), (bv_s, bv)):
                act.dma_start(dst, src).then_inc(small_in, 16)
            act.dma_start(rw_s, rw).then_inc(small_in, 16)
            act.dma_start(bo_s, bo.partition_broadcast(P)).then_inc(wide_in, 16)
            act.dma_start(rb_s, rb.partition_broadcast(P)).then_inc(small_in, 16)
            act.dma_start(attl_s, att_l.partition_broadcast(P)).then_inc(small_in, 16)
            act.dma_start(attr_s, att_r.partition_broadcast(P)).then_inc(small_in, 16)
            for t in range(T):
                act.wait_ge(xt_done, t + 1)
                a.activation(xnT[:, :, t * P:(t + 1) * P], bank[2 + t][:, :].rearrange("p (k c) -> p k c", k=KD),
                             ACT.Copy).then_inc(xnT_ok, 1)
            act.wait_ge(small_in, 16 * 7)
            for m in range(KD):
                act.wait_ge(q_done, m + 1)
                a.activation(qT[:, m, :], bank[(0, 1, 6, 7)[m]][:, :], ACT.Identity,
                             bias=bq_s[:, m:m + 1]).then_inc(qT_ok, 1)
            for m in range(KD):
                act.wait_ge(qk_done, m + 1)
                a.activation(qkT[:, m, :], bank[2 + m][:, :], ACT.Copy).then_inc(qkT_ok, 1)
            act.wait_ge(bkq_done, 1)
            a.activation(bkq, bank[0][:, 0:T], ACT.Copy).then_inc(bkq_ok, 1)

            with act.Fori(0, PAIRS) as i:
                act.wait_ge(nb_ok, i + 1)
                a.activation(pr, psum[:, 0:KEYS], ACT.Exp, bias=nb, scale=SCALE, accum_out=den).then_inc(exp_ok, 1)
                for n in (0, 2):
                    act.wait_ge(prt_done, i * NC + (n + 1))
                    a.activation(prT[:, 4 * n:4 * n + 4, :], bank[4][:, :].rearrange("p (j c) -> p j c", j=4),
                                 ACT.Copy).then_inc(prt_act, 1)
                act.wait_ge(at_done, i + 1)
                a.activation(aT[:, :, bass.ds(i * P, P)], bank[7][:, :].rearrange("p (k c) -> p k c", k=KD),
                             ACT.Copy).then_inc(aT_ok, 1)

            act.wait_ge(aT_ok, PAIRS)
            act.dma_start(gamma_s, gamma.partition_broadcast(P)).then_inc(wide_in, 16)
            act.dma_start(beta_s, beta.partition_broadcast(P)).then_inc(wide_in, 16)
            for m in range(KD):
                act.wait_ge(v_done, m + 1)
                a.activation(vT[:, m, :], bank[m][:, :], ACT.Identity, bias=bv_s[:, m:m + 1]).then_inc(vT_ok, 1)
            for t in range(T):
                act.wait_ge(ht_done, t + 1)
                a.activation(hT[:, :, t * P:(t + 1) * P], bank[t][:, :].rearrange("p (k c) -> p k c", k=KD),
                             ACT.Copy).then_inc(hT_ok, 1)
            for t in range(T):
                act.wait_ge(f_done, 2 * t + 2)
                a.activation(fr[:, t, :], bank[t][:, :], ACT.Copy).then_inc(fr_ok, 1)
            for t in range(T):
                act.wait_ge(arg_ok, t + 1)
                a.activation(att_tmp[:, t, :], att_tmp[:, t, :], ACT.Exp).then_inc(pexp_ok, 1)
            for t in range(T):
                for b2_ in range(2):
                    act.wait_ge(hs_done, 2 * t + b2_ + 1)
                    a.activation(hsT[:, :, t * P + b2_ * S:t * P + (b2_ + 1) * S],
                                 bank[4 + 2 * (t % 2) + b2_][:, 0:KD * S].rearrange("p (k c) -> p k c", k=KD),
                                 ACT.Copy).then_inc(hsT_ok, 1)
            for t in range(T):
                act.wait_ge(x2t_done, t + 1)
                a.activation(xT[:, :, t * P:(t + 1) * P], bank[t][:, :].rearrange("p (k c) -> p k c", k=KD),
                             ACT.Copy).then_inc(xT_ok, 1)
            act.wait_ge(top_ok, 1)
            a.activation(ew, ew, ACT.Exp).then_inc(ew_ok, 1)

            act.wait_ge(base_ok, 1)
            total = act.value_load(base_i[0:1, E:E + 1], min_val=1, max_val=CH_MAX)
            with act.Fori(0, total) as c:
                for u in range(2):
                    act.wait_ge(lin_ok, c * 2 + (u + 1))
                    a.activation(glu[u], glu[u], ACT.Silu).then_inc(silu_ok, 1)
                    act.wait_ge(hidt_done, c * 2 + (u + 1))
                    a.activation(hidT[:, u, :, :], bank[5 + u][:, :].rearrange("p (c n) -> p c n", c=4),
                                 ACT.Copy).then_inc(hidT_ok, 1)

        @block.tensor
        def _(pe):
            mm = nc.tensor.matmul

            def tr(dst, src, n=P):
                return nc.tensor.transpose(dst, src, ident[0:n, 0:n])

            def blocks(dst, lhs, rhs):
                for k in range(KD):
                    ins = mm(dst, lhs(k), rhs(k), start=(k == 0), stop=(k == KD - 1))
                return ins

            pe.wait_ge(const_ok, 1)
            for t in range(T):
                pe.wait_ge(xn_ok, t + 1)
                for k in range(KD):
                    ins = tr(bank[2 + t][:, k * P:(k + 1) * P], xn[:, t, k * P:(k + 1) * P])
                ins.then_inc(xt_done, 1)
            pe.wait_ge(xnT_ok, T)
            pe.wait_ge(wqk_in, 32)
            for m in range(KD):
                blocks(bank[(0, 1, 6, 7)[m]][:, :], lambda k: wq_s[:, k, m * P:(m + 1) * P], lambda k: xnT[:, k, :])\
                    .then_inc(q_done, 1)
            pe.wait_ge(qT_ok, KD)
            for m in range(KD):
                blocks(bank[2 + m][:, :], lambda k: wk_s[:, k, m * P:(m + 1) * P], lambda k: qT[:, k, :])\
                    .then_inc(qk_done, 1)
            for t in range(T):
                ins = blocks(bank[0][:, t:t + 1], lambda k: qT[:, k, t * P:(t + 1) * P], lambda k: bk_s[:, k:k + 1])
            ins.then_inc(bkq_done, 1)
            pe.wait_ge(qkT_ok, KD)
            pe.wait_ge(bkq_ok, 1)

            with pe.Fori(0, PAIRS) as i:
                hold(pe, qp_ok, i + 1)
                for n in range(NC):
                    hold(pe, ctxT_in[n], i * 16 + 16)
                    for k in range(KD):
                        for a_ in range(2):
                            ins = mm(psum[a_ * S:(a_ + 1) * S, n * 512:n * 512 + NCOLS[n]], qp[:, k, a_ * S:(a_ + 1) * S],
                                     ctxT[n][:, a_, k, :], start=(k == 0), stop=(k == KD - 1))
                    ins.then_inc(sc_done, 1)
                hold(pe, exp_ok, i + 1)
                for n in range(NC):
                    if n >= 2:
                        hold(pe, (prt_act, prt_dve)[n % 2], i * 2 + 1)
                    for j in range(4 * n, min(4 * n + 4, J)):
                        w_ = REST if j == JF else P
                        ins = tr(bank[4 + n % 2][0:w_, (j % 4) * P:(j % 4 + 1) * P], pr[:, j * P:j * P + w_])
                    ins.then_inc(prt_done, 1)
                hold(pe, ctx_in_s, i * 64 + 64)
                for j in range(J):
                    if j % 4 == 0:
                        n = j // 4
                        hold(pe, (prt_act, prt_dve)[n % 2], i * 2 + (n // 2 + 1))
                    w_ = REST if j == JF else P
                    for a_ in range(2):
                        ins = mm(bank[6][a_ * S:(a_ + 1) * S, :], prT[0:w_, j, a_ * S:(a_ + 1) * S], ctx[a_][0:w_, j, :],
                                 start=(j == 0), stop=(j == J - 1))
                ins.then_inc(av_done, 1)
                hold(pe, ao_ok, i + 1)
                for k in range(KD):
                    ins = tr(bank[7][:, k * P:(k + 1) * P], ao[:, k * P:(k + 1) * P])
                ins.then_inc(at_done, 1)

            pe.wait_ge(aT_ok, PAIRS)
            pe.wait_ge(wc_in, 16 * 5)
            for m in range(KD):
                blocks(bank[m][:, :], lambda k: wv_s[:, k, m * P:(m + 1) * P], lambda k: aT[:, k, :]).then_inc(v_done, 1)
            pe.wait_ge(vT_ok, KD)
            for t in range(T):
                blocks(bank[4 + t][:, :], lambda k: vT[:, k, t * P:(t + 1) * P], lambda k: wo_s[:, k, :]).then_inc(o_done, 1)
            for t in range(T):
                pe.wait_ge(h_ok, t + 1)
                for k in range(KD):
                    ins = tr(bank[t][:, k * P:(k + 1) * P], h_nat[:, t, k * P:(k + 1) * P])
                ins.then_inc(ht_done, 1)
            for t in range(T):
                pe.wait_ge(hT_ok, t + 1)
                blocks(bank[4 + t][:, :], lambda k: hT[:, k, t * P:(t + 1) * P], lambda k: wl_s[:, k, :]).then_inc(f_done, 1)
                blocks(bank[t][:, :], lambda k: hT[:, k, t * P:(t + 1) * P], lambda k: wr_s[:, k, :]).then_inc(f_done, 1)
            for t in range(T):
                pe.wait_ge(srs_ok, t + 1)
                tr(bank[4 + t][0:H, 0:P], sr[:, t, :]).then_inc(srT_done, 1)
                pe.wait_ge(mxl_ok, t + 1)
                mm(bank[4 + t][:, 256:256 + H], mxl[0:H, :], ident[0:H, 0:H], start=True, stop=True).then_inc(srm_done, 1)
            def self_scores(t):
                pe.wait_ge(spread_ok, t + 1)
                if t == 0:
                    pe.wait_ge(fr_ok, T)
                mm(bank[0][:, :], same, spread[:, 0, :, :].rearrange("p h n -> p (h n)"), start=True, stop=True)
                mm(bank[1][:, :], same, spread[:, 1, :, :].rearrange("p h n -> p (h n)"), start=True, stop=True).then_inc(st_done, 1)

            def self_weigh(t):
                pe.wait_ge(pexp_ok, t + 1)
                mm(bank[2 + t % 2][:, :], same, att_tmp[:, t, :], start=True, stop=True).then_inc(pden_done, 1)
                pe.wait_ge(pn_ok, t + 1)
                if t >= 2:
                    pe.wait_ge(hsT_ok, 2 * (t - 1))
                for b_ in range(2):
                    for h in range(H):
                        q = (h % 2) * HD
                        ins = mm(bank[4 + 2 * (t % 2) + b_][q:q + HD, (h // 2) * S:(h // 2 + 1) * S],
                                 fr[b_ * S:(b_ + 1) * S, t, h * HD:(h + 1) * HD],
                                 att_tmp[b_ * S:(b_ + 1) * S, t, h * S:(h + 1) * S], start=True, stop=True)
                    ins.then_inc(hs_done, 1)

            self_scores(0)
            for t in range(T):
                if t + 1 < T:
                    self_scores(t + 1)
                self_weigh(t)
            for t in range(T):
                pe.wait_ge(hsT_ok, 2 * t + 2)
                blocks(bank[t][:, :], lambda k: hsT[:, k, t * P:(t + 1) * P], lambda k: wf_s[:, k, :]).then_inc(wf_done, 1)
            for t in range(T):
                pe.wait_ge(xn2_ok, t + 1)
                for k in range(KD):
                    ins = tr(bank[t][:, k * P:(k + 1) * P], xn[:, t, k * P:(k + 1) * P])
                ins.then_inc(x2t_done, 1)
            for t in range(T):
                pe.wait_ge(xT_ok, t + 1)
                blocks(bank[4][:, t * E:(t + 1) * E], lambda k: xT[:, k, t * P:(t + 1) * P], lambda k: rw_s[:, k, :])\
                    .then_inc(lg_done, 1)
            pe.wait_ge(hot_ok, 1)
            for t in range(T):
                mm(bank[5][:, t * E:(t + 1) * E], below, both[:, t, :], start=True, stop=(t == 0))
                for u in range(t):
                    mm(bank[5][:, t * E:(t + 1) * E], ones, both[:, u, :], start=False, stop=(u == t - 1))
            for t in range(T):
                ins = mm(bank[5][:, T * E:(T + 1) * E], ones, both[:, t, :], start=(t == 0), stop=(t == T - 1))
            ins.then_inc(rank_done, 1)

            def turn_rows(n):
                hold(pe, xg_in, n)
                for k in range(KD):
                    ins = tr(bank[7][:, k * W:(k + 1) * W], xg[:, k * P:(k + 1) * P], W)
                ins.then_inc(xgt_done, 1)

            def up(r, q):
                for k in range(KD):
                    for a_ in range(2):
                        ins = mm(bank[q][a_ * W:(a_ + 1) * W, :], xgT[:, k, :], w1buf[r][:, q, a_, k, :],
                                 start=(k == 0), stop=(k == KD - 1))
                ins.then_inc(up_done, 1)

            def turn_hidden(c, u):
                pe.wait_ge(hid_ok, c * 2 + (u + 1))
                for n in range(4):
                    ins = tr(bank[5 + u][:, n * P:(n + 1) * P], hid[u][:, n * P:(n + 1) * P])
                ins.then_inc(hidt_done, 1)

            def down(u, n):
                for a_ in range(2):
                    ins = mm(bank[4][a_ * W:(a_ + 1) * W, :], hidT[:, u, n, a_ * W:(a_ + 1) * W],
                             w2buf[:, (u * 4 + n) * 2 + a_, :], start=(u == 0 and n == 0), stop=(u == 1 and n == 3))
                if u == 1 and n == 3:
                    ins.then_inc(down_done, 1)

            turn_rows(16)
            with pe.Fori(0, E // 2) as ep:
                for r in range(2):
                    lo, hi = chunk_range(pe, ep * 2 + r)
                    with pe.Fori(lo, hi) as c:
                        hold(pe, xgT_ok, c + 1)
                        for q in range(PIECES):
                            hold(pe, w1_in[r][q], ep * 16 + 16)
                            up(r, q)
                            if q == 2:
                                turn_hidden(c, 0)
                        hold(pe, w2_in[0], ep * 32 + (16 * r + 16))
                        hold(pe, hidT_ok, c * 2 + 1)
                        for n in range(4):
                            down(0, n)
                            if n == 2:
                                turn_hidden(c, 1)
                        turn_rows(c * 16 + 32)
                        hold(pe, w2_in[1], ep * 32 + (16 * r + 16))
                        hold(pe, hidT_ok, c * 2 + 2)
                        for n in range(4):
                            down(1, n)

        @block.vector
        def _(dve):
            v = nc.vector
            o = Order(dve, v_order)

            def norm_stats(n, src):
                t = n % T
                o.link(v.bn_stats(stats[:, t, :], src))
                o.link(v.bn_aggr(mv[:, t, :], stats[:, t, :]))
                v.tensor_scalar(mv[:, t, 1:2], mv[:, t, 1:2], EPS, None, ALU.add).then_inc(var_ok, 1)

            def normalise(n, dst, src):
                t = n % T
                dve.wait_ge(rstd_ok, n + 1)
                return v.tensor_scalar(dst, src, mv[:, t, 0:1], rstd[:, t:t + 1], ALU.subtract, ALU.mult)

            for t in range(T):
                if t == 0:
                    dve.wait_ge(x_in, 16 * T)
                norm_stats(t, xres[:, t, :])
            for t in range(T):
                normalise(t, xn[:, t, :], xres[:, t, :]).then_inc(xn_ok, 1)

            dve.wait_ge(bkq_ok, 1)
            with dve.Fori(0, PAIRS) as i:
                ob = Order(dve, row_order, i * 3)
                ob.link(v.tensor_copy(bkq1, bkq[:, bass.ds(i, 1)]))
                dve.wait_ge(sc_done, i * NC + NC)
                ob.link(v.tensor_reduce(mx, psum[:, 0:KEYS], AX.X, ALU.max))
                ob.link(v.tensor_tensor(mxr, mx, bkq1, ALU.add))
                v.tensor_scalar(nb, bkq1, mxr, SCALE, ALU.subtract, ALU.mult).then_inc(nb_ok, 1)
                dve.wait_ge(exp_ok, i + 1)
                v.reciprocal(rec, den).then_inc(rec_ok, 1)
                for n in (1, 3):
                    dve.wait_ge(prt_done, i * NC + (n + 1))
                    if n == 1:
                        v.tensor_copy(prT[:, 4:8, :], bank[5][:, :].rearrange("p (j c) -> p j c", j=4)).then_inc(prt_dve, 1)
                    else:
                        v.tensor_copy(prT[0:REST, JF, :], bank[5][0:REST, 0:P]).then_inc(prt_dve, 1)
                dve.wait_ge(av_done, i + 1)
                dve.wait_ge(rec_ok, i + 1)
                v.tensor_scalar(ao, bank[6][:, :], rec, None, ALU.mult).then_inc(ao_ok, 1)

            for t in range(T):
                dve.wait_ge(o_done, t + 1)
                dve.wait_ge(xb_ok, t + 1)
                o.link(v.tensor_tensor(xres[:, t, :], bank[4 + t][:, :], xres[:, t, :], ALU.add))
                norm_stats(T + t, xres[:, t, :])
                normalise(T + t, xn[:, t, :], xres[:, t, :]).then_inc(h_ok, 1)
            for t in range(T):
                for side, (att, dst) in enumerate(((attl_s, sl), (attr_s, sr))):
                    tmp = lk[side]
                    if side:
                        dve.wait_ge(fr_ok, t + 1)
                        o.link(v.scalar_tensor_tensor(out=tmp, in0=fr[:, t, :], scalar=0.01, in1=fr[:, t, :],
                                                      op0=ALU.mult, op1=ALU.max))
                    else:
                        dve.wait_ge(f_done, 2 * t + 1)
                        o.link(v.tensor_scalar(tmp, bank[4 + t][:, :], 0.01, None, ALU.mult))
                        o.link(v.tensor_tensor(tmp, bank[4 + t][:, :], tmp, ALU.max))
                    th = tmp.rearrange("p (h d) -> p h d", h=H)
                    o.link(v.tensor_tensor(th, th, att.unsqueeze(1).to_broadcast([P, H, HD]), ALU.mult))
                    ins = v.tensor_reduce(dst[:, t, :], th, AX.X, ALU.add)
                    if side:
                        ins.then_inc(srs_ok, 1)
                    else:
                        o.step(ins)
            o.settle()
            for t in range(T):
                dve.wait_ge(srT_done, t + 1)
                o.link(v.tensor_reduce(srx[0:H, :], bank[4 + t][0:H, 0:P].rearrange("h (b m) -> h b m", b=2), AX.X, ALU.max))
                v.tensor_copy(mxl[0:H, :].rearrange("h (b m) -> h b m", b=2),
                              srx[0:H, :].unsqueeze(2).to_broadcast([H, 2, S])).then_inc(mxl_ok, 1)
                dve.wait_ge(srm_done, t + 1)
                o.link(v.tensor_tensor(slm[:, t, :], sl[:, t, :], bank[4 + t][:, 256:256 + H], ALU.add))

            def spread_left(t):
                if t:
                    dve.wait_ge(st_done, t)
                wide = place.unsqueeze(1).to_broadcast([P, H, S])
                o.link(v.tensor_tensor(spread[:, 0, :, :], sl[:, t, :].unsqueeze(2).to_broadcast([P, H, S]), wide, ALU.mult))
                v.tensor_tensor(spread[:, 1, :, :], slm[:, t, :].unsqueeze(2).to_broadcast([P, H, S]), wide, ALU.mult)\
                    .then_inc(spread_ok, 1)

            spread_left(0)
            for t in range(T):
                dve.wait_ge(st_done, t + 1)
                dst = att_tmp[:, t, :]
                o.link(v.tensor_tensor(dst.rearrange("p (h n) -> p h n", h=H),
                                       bank[0][:, :].rearrange("p (h n) -> p h n", h=H),
                                       sr[:, t, :].unsqueeze(2).to_broadcast([P, H, S]), ALU.add))
                v.tensor_tensor(dst, dst, bank[1][:, :], ALU.subtract).then_inc(arg_ok, 1)
                if t + 1 < T:
                    dve.wait_ge(arg_ok, t + 1)
                    spread_left(t + 1)
                dve.wait_ge(pden_done, t + 1)
                o.link(v.reciprocal(lk[t % 2], bank[2 + t % 2][:, :]))
                v.tensor_tensor(dst, dst, lk[t % 2], ALU.mult).then_inc(pn_ok, 1)
            for t in range(T):
                dve.wait_ge(wf_done, t + 1)
                o.link(v.tensor_tensor(xn[:, t, :], bank[t][:, :], xn[:, t, :], ALU.add))
                norm_stats(2 * T + t, xn[:, t, :])
                normalise(2 * T + t, xn[:, t, :], xn[:, t, :]).then_inc(yn_ok, 1)
            for t in range(T):
                dve.wait_ge(x2_ok, t + 1)
                norm_stats(3 * T + t, xres[:, t, :])
                normalise(3 * T + t, xn[:, t, :], xres[:, t, :]).then_inc(xn2_ok, 1)

            dve.wait_ge(lg_done, T)
            wideE = lambda ap: ap.unsqueeze(2).to_broadcast([P, T, E])
            wideT = lambda ap: ap.unsqueeze(1).to_broadcast([P, T, E])
            o.link(v.tensor_tensor(lg, bank[4][:, 0:T * E].rearrange("p (t e) -> p t e", t=T), wideT(rb_s), ALU.add))

            def pick(src, best, hot):
                o.link(v.tensor_reduce(best, src, AX.X, ALU.max))
                o.link(v.tensor_tensor(eq, src, wideE(best), ALU.is_equal))
                o.link(v.tensor_scalar(eq, eq, -2.0 * E, 2.0 * E, ALU.mult, ALU.add))
                o.link(v.tensor_tensor(cand, eq, wideT(iota), ALU.add))
                o.link(v.tensor_reduce(idx, cand, AX.X, ALU.min))
                o.link(v.tensor_tensor(hot, wideT(iota), wideE(idx), ALU.is_equal))

            pick(lg, top[:, 0, :], oh1)
            o.link(v.tensor_scalar(lg2, oh1, LOWEST, None, ALU.mult))
            o.link(v.tensor_tensor(lg2, lg2, lg, ALU.add))
            pick(lg2, top[:, 1, :], oh2)
            v.tensor_tensor(both, oh1, oh2, ALU.add).then_inc(hot_ok, 1)
            v.tensor_tensor(ew, top[:, 1, :], top[:, 0, :], ALU.subtract).then_inc(top_ok, 1)
            dve.wait_ge(rank_done, 1)
            o.link(v.tensor_copy(cnt, bank[5][:, T * E:(T + 1) * E]))
            o.link(v.tensor_tensor(cmp7, cnt.unsqueeze(2).to_broadcast([P, E, 7]),
                                   over.unsqueeze(1).to_broadcast([P, E, 7]), ALU.is_gt))
            o.link(v.tensor_reduce(chs, cmp7, AX.X, ALU.add))
            o.link(v.tensor_scalar(chs, chs, 1.0, None, ALU.add))
            o.link(v.tensor_tensor(cmp9, chs.unsqueeze(1).to_broadcast([P, E + 1, E]), tri, ALU.mult))
            o.link(v.tensor_reduce(basef, cmp9, AX.X, ALU.add))
            v.tensor_copy(base_i[:, :], basef).then_inc(base_ok, 1)
            o.link(v.tensor_scalar(chs, basef[:, 0:E], float(W), None, ALU.mult))
            o.link(v.tensor_tensor(rank, bank[5][:, 0:T * E].rearrange("p (t e) -> p t e", t=T), wideT(chs), ALU.add))
            for k, hot in enumerate((oh1, oh2)):
                o.link(v.tensor_tensor(cand, hot, rank, ALU.mult))
                o.link(v.tensor_reduce(dst_f[:, k, :], cand, AX.X, ALU.add))
            v.tensor_copy(dest_i[:, :, :], dst_f).then_inc(dest_ok, 1)
            dve.wait_ge(ew_ok, 1)
            o.link(v.tensor_scalar(wsum, ew, 1.0, None, ALU.add))
            o.link(v.reciprocal(gate[:, 0, :], wsum))
            v.tensor_tensor(gate[:, 1, :], gate[:, 0, :], ew, ALU.mult).then_inc(gate_ok, 1)

            dve.wait_ge(xgt_done, 1)
            dve.wait_ge(dest_ok, 1)
            dve.wait_ge(gate_ok, 1)
            turned_rows = bank[7][:, 0:KD * W].rearrange("p (k c) -> p k c", k=KD)
            v.tensor_copy(xgT, turned_rows).then_inc(xgT_ok, 1)
            with dve.Fori(0, E // 2) as ep:
                for r in range(2):
                    lo, hi = chunk_range(dve, ep * 2 + r)
                    hold(dve, bias_in[r], ep * 48 + 48)
                    with dve.Fori(lo, hi) as c:
                        oc = Order(dve, sum_order, c * 3)
                        for u in range(2):
                            hold(dve, up_done, c * PIECES + (2 * u + 1))
                            v.tensor_tensor(glu[u], bank[2 * u][:, :], b1_s[r][:, 2 * u, :], ALU.add).then_inc(lin_ok, 1)
                            hold(dve, up_done, c * PIECES + (2 * u + 2))
                            oc.link(v.tensor_tensor(hid[u], bank[2 * u + 1][:, :], b1_s[r][:, 2 * u + 1, :], ALU.add))
                            dve.wait_ge(silu_ok, c * 2 + (u + 1))
                            v.tensor_tensor(hid[u], hid[u], glu[u], ALU.mult).then_inc(hid_ok, 1)
                        dve.wait_ge(xgt_done, c + 2)
                        v.tensor_copy(xgT, turned_rows).then_inc(xgT_ok, 1)
                        dve.wait_ge(y_stored, c * 16 + 16)
                        hold(dve, down_done, c + 1)
                        oc.link(v.tensor_tensor(yrow, bank[4][0:W, :], b2_s[r], ALU.add))
                        v.tensor_tensor(yrow, bank[4][W:P, :], yrow, ALU.add).then_inc(yrow_ok, 1)
            for t in range(T):
                dve.wait_ge(got_in[t], 32)
                for k in range(2):
                    v.scalar_tensor_tensor(out=xres[:, t, :], in0=got[:, k, t, :], scalar=gate[:, k, t:t + 1],
                                           in1=xres[:, t, :], op0=ALU.mult, op1=ALU.add).then_inc(res_ok, 1)
                    if k == 0:
                        dve.wait_ge(res_ok, 2 * t + 1)


def kernel(**inputs):
    import numpy as np
    import concourse.bacc as bacc
    from concourse.bass_utils import run_bass_kernel_spmd

    a = {k: np.asarray(v) for k, v in inputs.items()}

    def cols(vec):
        return vec.reshape(-1, P).T

    def rows_of(mat):
        return mat.reshape(-1, P, mat.shape[1]).transpose(1, 0, 2)

    w1 = a["L0_ffn_w1"].reshape(E, 2, 2, 2, 512, KD, P)
    b1 = a["L0_ffn_b1"].reshape(E, 2, 2, 2, 512)
    w2 = a["L0_ffn_w2"].reshape(E, D, 2, 2, 4, P)
    c = a["ctx_1024"]
    head = c[:, :JF * P].reshape(B, P, JF, D).transpose(0, 3, 2, 1).reshape(B, D, JF * P)
    cT = np.concatenate([head, c[:, JF * P:].transpose(0, 2, 1)], axis=2).reshape(PAIRS, 2, KD, P, KEYS)
    cT = cT.transpose(0, 3, 1, 2, 4)
    cT = np.concatenate([cT[..., n * 512:n * 512 + NCOLS[n]].reshape(PAIRS, P, -1) for n in range(NC)], axis=2)
    arrays = {
        "x": a["x"].reshape(TOK, D),
        "ctx": a["ctx_1024"],
        "ctxT": cT,
        "wq": rows_of(a["L0_xattn_Wq"].T), "bq": cols(a["L0_xattn_bq"]),
        "wk": rows_of(a["L0_xattn_Wk"]), "bk": cols(a["L0_xattn_bk"]),
        "wv": rows_of(a["L0_xattn_Wv"].T), "bv": cols(a["L0_xattn_bv"]),
        "wo": rows_of(a["L0_xattn_Wo"].T), "bo": a["L0_xattn_bo"],
        "wl": rows_of(a["L0_attn_Wl"].T), "wr": rows_of(a["L0_attn_Wr"].T),
        "att_l": a["L0_attn_att_l"].reshape(HD), "att_r": a["L0_attn_att_r"].reshape(HD),
        "wf": rows_of(a["L0_attn_Wf"].T), "gamma": a["L0_attn_ln_gamma"], "beta": a["L0_attn_ln_beta"],
        "rw": rows_of(a["L0_ffn_router_w"].T), "rb": a["L0_ffn_router_b"],
        "w1": w1.transpose(0, 6, 3, 1, 2, 5, 4).reshape(E, P, PIECES * 2 * KD * 512),
        "b1": b1.transpose(0, 2, 3, 1, 4).reshape(E, 2, PIECES * 512),
        "w2": w2.transpose(0, 5, 3, 4, 2, 1).reshape(E, P, M2 * D),
        "b2": a["L0_ffn_b2"],
    }
    nc = bacc.Bacc("TRN2", target_bir_lowering=False, num_devices=1)
    ins, args = {}, []
    for name, arr in arrays.items():
        arr = np.ascontiguousarray(arr)
        ins[f"in_{name}"] = arr
        args.append(nc.dram_tensor(f"in_{name}", arr.shape, mybir.dt.from_np(arr.dtype), kind="ExternalInput").ap())
    args.append(nc.dram_tensor("out", (TOK, D), F32, kind="ExternalOutput").ap())
    perceiver_layer(nc, *args)
    r = run_bass_kernel_spmd(nc, [ins], core_ids=[0])
    return r.results[0]["out"].reshape(B, S, D)
```

```python
import concourse.bass as bass
from concourse import mybir
from contextlib import ExitStack

F32 = mybir.dt.float32
I32 = mybir.dt.int32
U32 = mybir.dt.uint32
ALU = mybir.AluOpType
ACT = mybir.ActivationFunctionType
AX = mybir.AxisListType

P = 128
B, S, D = 8, 64, 512
KEYS = 1601
TOK = B * S
T = TOK // P
KD = D // P
JF = KEYS // P
REST = KEYS - JF * P
J = JF + 1
H, HD = 8, 64
E, FF = 8, 2048
M2 = FF // P
W = 64
CH_MAX = 2 * TOK // W + E
PAIRS = B // 2
BIG = CH_MAX * E
NC = (KEYS + 511) // 512
NCOLS = [min(512, KEYS - n * 512) for n in range(NC)]
PIECES = 4
SCALE = 1.0 / float(D / 16) ** 0.5
EPS = 1e-5
LOWEST = -3.0e38


class Order:

    def __init__(self, eng, sem, base=0):
        self.eng, self.sem, self.base, self.n = eng, sem, base, 0

    def step(self, ins):
        self.n += 1
        ins.then_inc(self.sem, 1)
        return self.n

    def settle(self, n=None):
        self.eng.wait_ge(self.sem, self.base + (self.n if n is None else n))

    def link(self, ins):
        self.step(ins)
        self.settle()


def perceiver_layer(nc, x, ctx_in, ctxT_in_, wq, bq, wk, bk, wv, bv, wo, bo, wl, wr, att_l, att_r, wf, gamma, beta,
                    rw, rb, w1, b1, w2, b2, out):
    es = ExitStack()

    def sem(name):
        return es.enter_context(nc.semaphore(name))

    with es:
        NW1 = M2 * 2 * KD * P
        NW2 = M2 * D
        NARENA = 53156
        arena = es.enter_context(nc.sbuf_tensor("arena", [P, NARENA], F32))
        psum = es.enter_context(nc.psum_tensor("psum", [P, 8 * 512], F32))
        bank = [psum[:, i * 512:(i + 1) * 512] for i in range(8)]
        base_i = es.enter_context(nc.sbuf_tensor("base_i", [P, 3, E + 1], I32))
        dest_i = es.enter_context(nc.sbuf_tensor("dest_i", [P, 2, T], I32))
        rows_in = nc.dram_tensor("rows_in", [(CH_MAX + 2) * W, D], F32, kind="Internal").ap()
        rows_out = nc.dram_tensor("rows_out", [(CH_MAX + 2) * W, D], F32, kind="Internal").ap()

        def area(start, *shape):
            n = 1
            for s in shape:
                n *= s
            assert start + n <= NARENA, start + n
            v = arena[:, start:start + n]
            if len(shape) == 1:
                return v
            names = "abcd"[:len(shape)]
            return v.rearrange(f"p ({' '.join(names)}) -> p {' '.join(names)}",
                               **dict(zip(names[1:], shape[1:])))

        W1A, W2A, W1B = 0, NW1, NW1 + NW2
        w1buf = [area(W1A, PIECES, 2, KD, 512), area(W1B, PIECES, 2, KD, 512)]
        w2buf = area(W2A, M2, D)
        NT = 2 * KD * KEYS
        NCTX = J * D
        ctxT = [area(n * 2 * KD * 512, 2, KD, NCOLS[n]) for n in range(NC)]
        ctx = [area(NT + i * NCTX, J, D) for i in range(2)]
        at = NT + 2 * NCTX

        def take(*shape):
            nonlocal at
            n = 1
            for d_ in shape:
                n *= d_
            at += n
            return area(at - n, *shape)

        wv_s, wo_s, wl_s, wr_s, wf_s = (take(KD, D) for _ in range(5))
        wq_s, wk_s, xnT = wl_s, wr_s, wf_s
        wvo = wv_s
        pr = take(KEYS)
        ao = take(D)
        place = take(S)
        same = take(P)
        zeros = take(P)
        qkT = take(KD, TOK)
        x2T = qkT
        assert at <= W1B + NW1, at
        at = W1B + NW1
        xres = take(T, D)
        xn = take(T, D)
        ident = take(P)
        gate = take(2, T)
        shared = at
        gamma_s, beta_s = take(D), take(D)
        qp = take(KD, P)
        qT = area(at, KD, TOK)
        hsT, h_nat, hT, att_p = take(KD, P), take(D), take(KD, P), take(D)
        fr = take(H, HD + 1)
        wide = [take(D) for _ in range(2)]
        yn = att_p
        hs_nat = wide[0]
        bo_s = wide[0]
        bv_w = wide[1].rearrange("p (k c) -> p k c", k=KD)
        aT = hT
        ones = take(P)
        below = take(P)
        bq_s, bk_s, bv_s = take(KD), take(KD), take(KD)
        count9, iota2, over, early = take(E + 1), take(E), take(E), take(E)
        iota = count9[:, 0:E]
        rb_s, rw_s = take(E), take(KD, E)
        attl_s, attr_s = take(HD), take(HD)
        stats, mv, rstd, half = take(T, 6), take(T, 2), take(T), take(1)
        bkq = take(T)
        bkq1, mx, mxr, nb, den, rec = (take(1) for _ in range(6))
        hden = take(H)
        sl, sr, slm, srx = take(H), take(H), take(H), take(2)
        lg = take(T, E)
        over_prT = at
        prT = take(J, P)
        endB = at
        at = over_prT
        mxl = wide[1][:, 0:P]
        eq, cand, lg2, rank = (take(T, E) for _ in range(4))
        hot = take(2, T, E)
        cand2 = take(2, T, E)
        both = take(T + 1, E)
        top = take(2, T)
        idx, ew, wsum = take(T), take(T), take(T)
        dst_f = take(2, T)
        chs, basef = take(E), take(3, E + 1)
        cmp8, before, cmp9 = take(E, E), take(E, E), take(E + 1, E)
        key, first, pos = take(E), take(E), take(E)
        endC = at
        at = shared
        b1_s = [take(PIECES, 512) for _ in range(2)]
        cols = take(D)
        b2_s = [cols[0:W, :], take(D)[0:W, :]]
        yrow = cols[W:P, :]
        xg, landed = take(D)[0:W, :], take(D)[0:W, :]
        xgT = take(KD, W)
        glu = [xn[:, 2, :], take(512)]
        hid = [xn[:, 3, :], take(512)]
        hidT = xn[:, 0:2, :].rearrange("p u (c n) -> p u c n", c=4)
        endD = at
        assert max(endB, endC, endD) <= NARENA, (endB, endC, endD)
        got = area(W1A, 2, T, D)

        x_in = [sem(f"x_in{t}") for t in range(T)]
        wq_in, wk_in = sem("wq_in"), sem("wk_in")
        small_in = sem("small_in")
        bo_in, gb_in = sem("bo_in"), sem("gb_in")
        ctxT_in = [sem(f"ctxT_in{n}") for n in range(NC)]
        ctx_in_s = sem("ctx_in")
        wc_in = sem("wc_in")
        ident_ok, const_ok = sem("ident_ok"), sem("const_ok")
        p_order, v_order = sem("p_order"), sem("v_order")
        var_ok = [sem(f"var{n}_ok") for n in range(4)]
        rstd_ok = [sem(f"rstd{n}_ok") for n in range(4)]
        xn_ok, xb_ok = sem("xn_ok"), sem("xb_ok")
        xt_done, xnT_ok = sem("xt_done"), sem("xnT_ok")
        q_done, qT_ok = sem("q_done"), sem("qT_ok")
        qk_done, qkT_ok = sem("qk_done"), sem("qkT_ok")
        bkq_done, bkq_ok = sem("bkq_done"), sem("bkq_ok")
        qp_ok, sc_done, row_order, nb_ok, exp_ok = sem("qp_ok"), sem("sc_done"), sem("row_order"), sem("nb_ok"), sem("exp_ok")
        prt_done, prT_ok = sem("prt_done"), sem("prT_ok")
        av_done, rec_ok, ao_ok, at_done, aT_ok = sem("av_done"), sem("rec_ok"), sem("ao_ok"), sem("at_done"), sem("aT_ok")
        wvo_in, bv_ok, bvo_done, bo_ok = sem("wvo_in"), sem("bv_ok"), sem("bvo_done"), sem("bo_ok")
        wvo_done, wvo_ok, x1b_ok = sem("wvo_done"), sem("wvo_ok"), sem("x1b_ok")
        o_done = sem("o_done")
        h_ok, ht_done, hT_ok = sem("h_ok"), sem("ht_done"), sem("hT_ok")
        fl_done, fr_done, fr_ok = sem("fl_done"), sem("fr_done"), sem("fr_ok")
        side_order, sr_ok, srT_done, mxl_ok, srm_done = sem("side_order"), sem("sr_ok"), sem("srT_done"), sem("mxl_ok"), sem("srm_done")
        spread_ok, st_done, arg_ok, pexp_ok = sem("spread_ok"), sem("st_done"), sem("arg_ok"), sem("pexp_ok")
        hs_done, hn_ok, hst_done, hsT_ok = sem("hs_done"), sem("hn_ok"), sem("hst_done"), sem("hsT_ok")
        wf_done = sem("wf_done")
        n_order, y_free = sem("n_order"), sem("y_free")
        xn2_ok, x2t_done, xT_ok = sem("xn2_ok"), sem("x2t_done"), sem("xT_ok")
        lg_done, top_ok, ew_ok, hot_ok, rank_done = sem("lg_done"), sem("top_ok"), sem("ew_ok"), sem("hot_ok"), sem("rank_done")
        base_ok, dest_ok, gate_ok = sem("base_ok"), sem("dest_ok"), sem("gate_ok")
        zero_ok, filled = sem("zero_ok"), sem("filled")
        scattered = sem("scattered")
        w1_in = [[sem(f"w1_in{i}_{n}") for n in range(PIECES)] for i in range(2)]
        w2_in = [sem(f"w2_in{n}") for n in range(2)]
        bias_in = [sem(f"bias_in{i}") for i in range(2)]
        xg_in, landed_in, xg_ok = sem("xg_in"), sem("landed_in"), sem("xg_ok")
        xgt_done, xgT_ok = sem("xgt_done"), sem("xgT_ok")
        up_done, lin_ok, silu_ok, hid_ok = sem("up_done"), sem("lin_ok"), sem("silu_ok"), sem("hid_ok")
        hidt_done, hidT_ok, down_done = sem("hidt_done"), sem("hidT_ok"), sem("down_done")
        sum_order, yrow_ok, y_stored = sem("sum_order"), sem("yrow_ok"), sem("y_stored")
        got_in = [sem(f"got_in{t}") for t in range(T)]
        res_ok, stored = sem("res_ok"), sem("stored")

        passed = {e.engine: sem(f"passed_{n}") for n, e in (("pe", nc.tensor), ("pool", nc.gpsimd), ("dve", nc.vector))}

        block = es.enter_context(nc.Block())

        def hold(eng, sem_, value):
            eng.wait_ge(sem_, value)
            eng.sem_inc(passed[eng.engine], 1)

        def chunk_range(eng, e):
            lo = eng.value_load(base_i[0:1, 0, bass.ds(e, 1)], min_val=0, max_val=CH_MAX - 1)
            hi = eng.value_load(base_i[0:1, 0, bass.ds(e + 1, 1)], min_val=1, max_val=CH_MAX)
            return lo, hi

        def expert_at(eng, position):
            return eng.value_load(base_i[0:1, 2, bass.ds(position, 1)], min_val=0, max_val=E - 1)

        def load_down(eng, e):
            for n in range(2):
                eng.dma_start(w2buf[:, n * (M2 // 2):(n + 1) * (M2 // 2), :].rearrange("p m d -> p (m d)"),
                             w2[bass.ds(e, 1), :, n * (NW2 // 2):(n + 1) * (NW2 // 2)].rearrange("o p c -> (o p) c"))\
                  .then_inc(w2_in[n], 16)

        def load_biases(eng, e, r):
            for a_ in range(2):
                eng.dma_start(b1_s[r][a_ * W:(a_ + 1) * W, :, :].rearrange("p q c -> p (q c)"),
                             b1[bass.ds(e, 1), a_, :].rearrange("o c -> (o c)").partition_broadcast(W)).then_inc(bias_in[r], 16)
            eng.dma_start(b2_s[r], b2[bass.ds(e, 1), :].rearrange("o c -> (o c)").partition_broadcast(W)).then_inc(bias_in[r], 16)

        @block.sync
        def _(sp):
            for t in range(T):
                sp.dma_start(xres[:, t, :], x[t * P:(t + 1) * P, :]).then_inc(x_in[t], 16)
            sp.dma_start(wq_s, wq).then_inc(wq_in, 16)
            sp.dma_start(wk_s, wk).then_inc(wk_in, 16)

            def load_turned(i, n):
                o_ = n * 2 * KD * 512
                w_ = 2 * KD * NCOLS[n]
                sp.dma_start(ctxT[n].rearrange("p a k c -> p (a k c)"),
                             ctxT_in_[bass.ds(i, 1), :, o_:o_ + w_].rearrange("o p c -> (o p) c")).then_inc(ctxT_in[n], 16)

            def load_rows(i):
                for a_ in range(2):
                    rows = ctx_in[bass.ds(i * 2 + a_, 1), :, :].rearrange("o k d -> (o k) d")
                    sp.dma_start(ctx[a_][:, 0:JF, :],
                                 rows[0:JF * P, :].rearrange("(p j) d -> p j d", j=JF)).then_inc(ctx_in_s, 16)
                    sp.dma_start(ctx[a_][0:REST, JF, :], rows[JF * P:KEYS, :]).then_inc(ctx_in_s, 16)

            for n in range(NC):
                load_turned(0, n)
            sp.dma_start(wv_s, wv).then_inc(wvo_in, 16)
            sp.dma_start(wo_s, wo).then_inc(wvo_in, 16)
            load_rows(0)
            sp.wait_ge(bkq_done, 1)
            for src, dst in ((wl, wl_s), (wr, wr_s), (wf, wf_s)):
                sp.dma_start(dst, src).then_inc(wc_in, 16)
            with sp.Fori(1, PAIRS) as i:
                for n in range(NC):
                    sp.wait_ge(sc_done, i * NC + (n + 1 - NC))
                    load_turned(i, n)
                sp.wait_ge(av_done, i)
                load_rows(i)

            def load_weights(e, r, pieces, last=None):
                for n in pieces:
                    if last is not None:
                        sp.wait_ge(up_done, last * PIECES + (n + 1))
                    sp.dma_start(w1buf[r][:, n, :, :, :].rearrange("p a k c -> p (a k c)"),
                                 w1[bass.ds(e, 1), :, n * (NW1 // PIECES):(n + 1) * (NW1 // PIECES)].rearrange("o p c -> (o p) c"))\
                      .then_inc(w1_in[r][n], 16)

            sp.wait_ge(const_ok, 1)
            wide_zeros = zeros.unsqueeze(1).to_broadcast([P, (CH_MAX + 2) * W * D // (P * P), P])
            for table in (rows_in, rows_out):
                sp.dma_start(table.rearrange("(p m) (k c) -> p (m k) c", p=P, c=P), wide_zeros).then_inc(filled, 16)
            sp.wait_ge(av_done, PAIRS)
            load_weights(0, 0, range(PIECES))
            load_down(sp, 0)
            sp.wait_ge(o_done, T)
            load_weights(1, 1, [0])
            sp.wait_ge(fl_done, T)
            load_weights(1, 1, [1])
            sp.wait_ge(wf_done, T)
            load_weights(1, 1, [2])
            sp.wait_ge(lg_done, T)
            sp.wait_ge(filled, 32)
            sp.wait_ge(xg_in, 16)
            load_weights(1, 1, [3])
            sp.wait_ge(base_ok, 1)
            with sp.Fori(0, E // 2 - 1) as ep:
                for r in range(2):
                    lo, _ = chunk_range(sp, ep * 2 + r)
                    last = sp.value_load(base_i[0:1, 1, bass.ds(ep * 2 + (r + 1), 1)], min_val=0, max_val=CH_MAX - 1)
                    coming = expert_at(sp, ep * 2 + (r + 2))
                    sp.wait_ge(yrow_ok, lo + 1)
                    load_weights(coming, r, range(PIECES), last)
            for t in range(T):
                sp.wait_ge(res_ok, 2 * (t + 1))
                sp.dma_start(out[t * P:(t + 1) * P, :], xres[:, t, :]).then_inc(stored, 16)
            sp.wait_ge(stored, 16 * T)

        @block.gpsimd
        def _(pool):
            g = nc.gpsimd
            o = Order(pool, p_order)

            def layer_rstd(kind, n, col):
                pool.wait_ge(var_ok[kind], n + 1)
                g.tensor_tensor(rstd[:, col:col + 1], mv[:, col, 1:2], half, ALU.pow).then_inc(rstd_ok[kind], 1)

            o.link(g.memset(half, -0.5))
            o.link(g.memset(ident, 0.0))
            g.affine_select(out=ident, in_=ident, compare_op=ALU.not_equal, fill=1.0, base=0,
                            pattern=[[-1, P]], channel_multiplier=1).then_inc(ident_ok, 1)
            for n in range(T):
                layer_rstd(0, n, n)
            o.link(g.memset(ones, 1.0))
            o.link(g.memset(fr[:, :, HD:HD + 1], 1.0))
            o.link(g.memset(same, 0.0))
            o.link(g.memset(below, 1.0))
            o.link(g.memset(place, 0.0))
            for e in range(E):
                o.link(g.memset(count9[:, e:e + 1], float(e)))
                o.link(g.memset(early[:, e:e + 1], float(BIG * (2 - e) if e < 2 else -e)))
                o.link(g.memset(iota2[:, e:e + 1], float(e + 2 * E)))
                o.link(g.memset(over[:, e:e + 1], float(W * e) if e else -1.0))
            o.settle()
            o.link(g.affine_select(out=below, in_=below, compare_op=ALU.is_ge, fill=0.0, base=-1,
                                   pattern=[[1, P]], channel_multiplier=-1))
            o.link(g.affine_select(out=place, in_=place, compare_op=ALU.not_equal, fill=1.0, base=0,
                                   pattern=[[-1, S]], channel_multiplier=1))
            o.link(g.affine_select(out=place, in_=place, compare_op=ALU.not_equal, fill=1.0, base=-S,
                                   pattern=[[-1, S]], channel_multiplier=1))
            for i in range(2):
                o.link(g.memset(same[i * S:(i + 1) * S, i * S:(i + 1) * S], 1.0))
            o.link(g.memset(count9[:, E:E + 1], float(E)))
            g.memset(zeros, 0.0).then_inc(const_ok, 1)

            pool.wait_ge(small_in, 16 * 7)
            g.tensor_copy(bv_w, bv_s.unsqueeze(2).to_broadcast([P, KD, P])).then_inc(bv_ok, 1)

            def queries(i):
                g.tensor_copy(qp, qkT[:, :, bass.ds(i * P, P)]).then_inc(qp_ok, 1)

            def tile_rows(ap, t):
                return ap[:, bass.ds(t, 1), :].rearrange("p o d -> p (o d)")

            def tile_c(t, more):
                layer_rstd(1, t, 1)
                if more:
                    pool.wait_ge(sc_done, t * NC + 2 * NC)
                    queries(t + 2)
                pool.wait_ge(h_ok, t + 1)
                rows = tile_rows(xres, t)
                g.tensor_tensor(rows, rows, beta_s, ALU.add).then_inc(x1b_ok, 1)
                layer_rstd(2, t, 2)
                layer_rstd(3, t, 3)

            pool.wait_ge(qkT_ok, KD)
            queries(0)
            pool.wait_ge(sc_done, NC)
            queries(1)
            pool.wait_ge(bo_ok, 1)
            pool.wait_ge(xn_ok, T)
            for t in range(T):
                g.tensor_tensor(xres[:, t, :], xres[:, t, :], bo_s, ALU.add).then_inc(xb_ok, 1)
            pool.wait_ge(gb_in, 32)
            with pool.Fori(0, PAIRS - 2) as t:
                tile_c(t, True)
            tile_c(PAIRS - 2, False)
            tile_c(PAIRS - 1, False)
            pool.wait_ge(filled, 32)
            pool.wait_ge(dest_ok, 1)
            pool.wait_ge(xn2_ok, T)
            for k in range(2):
                for t in range(T):
                    pool.indirect_dma_start(
                        out=rows_in, out_offset=bass.IndirectOffsetOnAxis(ap=dest_i[:, k, t:t + 1].bitcast(U32), axis=0),
                        in_=xn[:, t, :], in_offset=None).then_inc(scattered, 16)
            pool.wait_ge(gate_ok, 1)
            pool.wait_ge(scattered, 16 * 2 * T)
            pool.dma_start(xg, rows_in[0:W, :]).then_inc(xg_in, 16)
            g.memset(yrow, 0.0).then_inc(zero_ok, 1)
            pool.wait_ge(zero_ok, 1)
            pool.dma_start(rows_out[(CH_MAX + 1) * W:(CH_MAX + 2) * W, :], yrow).then_inc(y_stored, 16)
            pool.dma_start(landed, rows_in[W:2 * W, :]).then_inc(landed_in, 16)

            pool.wait_ge(base_ok, 1)
            total = pool.value_load(base_i[0:1, 0, E:E + 1], min_val=1, max_val=CH_MAX)
            with pool.Fori(0, total) as c:
                pool.wait_ge(landed_in, c * 16 + 16)
                hold(pool, xgt_done, c + 1)
                g.tensor_copy(xg, landed).then_inc(xg_ok, 1)
                pool.wait_ge(xg_ok, c + 1)
                pool.dma_start(landed, rows_in[bass.ds(c * W + 2 * W, W), :]).then_inc(landed_in, 16)
                pool.wait_ge(yrow_ok, c + 1)
                pool.dma_start(rows_out[bass.ds(c * W, W), :], yrow).then_inc(y_stored, 16)
            hold(pool, y_stored, (total + 1) * 16)
            for t in range(T):
                for k in range(2):
                    pool.indirect_dma_start(
                        out=got[:, k, t, :], out_offset=None, in_=rows_out,
                        in_offset=bass.IndirectOffsetOnAxis(ap=dest_i[:, k, t:t + 1].bitcast(U32), axis=0)).then_inc(got_in[t], 16)

        @block.scalar
        def _(act):
            a = nc.scalar
            for dst, src in ((bq_s, bq), (bk_s, bk), (bv_s, bv)):
                act.dma_start(dst, src).then_inc(small_in, 16)
            act.dma_start(rw_s, rw).then_inc(small_in, 16)
            act.dma_start(bo_s, bo.partition_broadcast(P)).then_inc(bo_in, 16)
            act.dma_start(rb_s, rb.partition_broadcast(P)).then_inc(small_in, 16)
            act.dma_start(attl_s, att_l.partition_broadcast(P)).then_inc(small_in, 16)
            act.dma_start(attr_s, att_r.partition_broadcast(P)).then_inc(small_in, 16)
            act.dma_start(gamma_s, gamma.partition_broadcast(P)).then_inc(gb_in, 16)
            act.dma_start(beta_s, beta.partition_broadcast(P)).then_inc(gb_in, 16)
            for t in range(T):
                act.wait_ge(xt_done, t + 1)
                a.activation(xnT[:, :, t * P:(t + 1) * P], bank[2 + t][:, :].rearrange("p (k c) -> p k c", k=KD),
                             ACT.Copy).then_inc(xnT_ok, 1)
            act.wait_ge(small_in, 16 * 7)
            for m in range(KD):
                act.wait_ge(q_done, m + 1)
                a.activation(qT[:, m, :], bank[(0, 1, 6, 7)[m]][:, :], ACT.Identity,
                             bias=bq_s[:, m:m + 1]).then_inc(qT_ok, 1)
            for m in range(KD):
                act.wait_ge(qk_done, m + 1)
                a.activation(qkT[:, m, :], bank[2 + m][:, :], ACT.Copy).then_inc(qkT_ok, 1)
            act.wait_ge(bkq_done, 1)
            a.activation(bkq, bank[0][:, 0:T], ACT.Copy).then_inc(bkq_ok, 1)

            def wide_exp(i):
                act.wait_ge(nb_ok, i + 1)
                a.activation(pr, psum[:, 0:KEYS], ACT.Exp, bias=nb, scale=SCALE, accum_out=den).then_inc(exp_ok, 1)

            def turned_exps(i):
                for n in range(NC):
                    act.wait_ge(prt_done, i * NC + (n + 1))
                    if n < NC - 1:
                        ins = a.activation(prT[:, 4 * n:4 * n + 4, :], bank[n].rearrange("p (j c) -> p j c", j=4), ACT.Copy)
                    else:
                        ins = a.activation(prT[0:REST, JF, :], bank[n][0:REST, 0:P], ACT.Copy)
                    ins.then_inc(prT_ok, 1)

            def turned(dst, src, done, n, ok):
                act.wait_ge(done, n)
                a.activation(dst, src.rearrange("p (k c) -> p k c", k=KD), ACT.Copy).then_inc(ok, 1)

            def turned_x2(t):
                turned(x2T[:, :, t * P:(t + 1) * P], bank[t], x2t_done, t + 1, xT_ok)

            def right_side(t):
                act.wait_ge(fr_done, t + 1)
                a.activation(fr[:, :, 0:HD], bank[7].rearrange("p (h d) -> p h d", h=H), ACT.Copy).then_inc(fr_ok, 1)

            def heads(t):
                act.wait_ge(arg_ok, t + 1)
                a.activation(att_p, att_p, ACT.Exp).then_inc(pexp_ok, 1)
                turned(hsT, bank[5], hst_done, t + 1, hsT_ok)

            wide_exp(0)
            act.wait_ge(wvo_done, KD)
            for m in range(KD):
                a.activation(wvo[:, m, :], bank[4 + m], ACT.Copy).then_inc(wvo_ok, 1)
            turned_exps(0)
            turned(aT, bank[7], at_done, 1, aT_ok)
            with act.Fori(1, PAIRS) as i:
                turned(hT, bank[5], ht_done, i, hT_ok)
                wide_exp(i)
                right_side(i - 1)
                turned_exps(i)
                heads(i - 1)
                turned(aT, bank[7], at_done, i + 1, aT_ok)
            for t in range(T - 1):
                turned_x2(t)
            turned(hT, bank[5], ht_done, T, hT_ok)
            right_side(PAIRS - 1)
            heads(PAIRS - 1)
            turned_x2(T - 1)
            act.wait_ge(top_ok, 1)
            a.activation(ew, ew, ACT.Exp).then_inc(ew_ok, 1)

            act.wait_ge(gate_ok, 1)
            act.wait_ge(scattered, 16 * 2 * T)
            act.wait_ge(xg_in, 16)
            for e in range(2):
                for a_ in range(2):
                    act.dma_start(b1_s[e][a_ * W:(a_ + 1) * W, :, :].rearrange("p q c -> p (q c)"),
                                  b1[e, a_, :].partition_broadcast(W)).then_inc(bias_in[e], 16)
                act.dma_start(b2_s[e], b2[e, :].partition_broadcast(W)).then_inc(bias_in[e], 16)

            act.wait_ge(base_ok, 1)

            def expert(position):
                lo, hi = chunk_range(act, position)
                with act.Fori(lo, hi) as c:
                    for u in range(2):
                        act.wait_ge(lin_ok, c * 2 + (u + 1))
                        a.activation(glu[u], glu[u], ACT.Silu).then_inc(silu_ok, 1)
                        act.wait_ge(hidt_done, c * 2 + (u + 1))
                        a.activation(hidT[:, u, :, :], bank[5 + u][:, :].rearrange("p (c n) -> p c n", c=4),
                                     ACT.Copy).then_inc(hidT_ok, 1)
                return hi

            def next_down(e, hi):
                act.wait_ge(down_done, hi)
                load_down(act, e)

            with act.Fori(0, E // 2 - 1) as ep:
                for r in range(2):
                    next1, next2 = expert_at(act, ep * 2 + (r + 1)), expert_at(act, ep * 2 + (r + 2))
                    hi = expert(ep * 2 + r)
                    next_down(next1, hi)
                    act.wait_ge(yrow_ok, hi)
                    load_biases(act, next2, r)
            next1 = expert_at(act, E - 1)
            hi = expert(E - 2)
            next_down(next1, hi)
            expert(E - 1)

        @block.tensor
        def _(pe):
            mm = nc.tensor.matmul

            def tr(dst, src, n=P):
                return nc.tensor.transpose(dst, src, ident[0:n, 0:n])

            def blocks(dst, lhs, rhs):
                for k in range(KD):
                    ins = mm(dst, lhs(k), rhs(k), start=(k == 0), stop=(k == KD - 1))
                return ins

            pe.wait_ge(ident_ok, 1)
            for t in range(T):
                pe.wait_ge(xn_ok, t + 1)
                for k in range(KD):
                    ins = tr(bank[2 + t][:, k * P:(k + 1) * P], xn[:, t, k * P:(k + 1) * P])
                ins.then_inc(xt_done, 1)
            pe.wait_ge(xnT_ok, T)
            pe.wait_ge(wq_in, 16)
            for m in range(KD):
                blocks(bank[(0, 1, 6, 7)[m]][:, :], lambda k: wq_s[:, k, m * P:(m + 1) * P], lambda k: xnT[:, k, :])\
                    .then_inc(q_done, 1)
            pe.wait_ge(qT_ok, KD)
            pe.wait_ge(wk_in, 16)
            for m in range(KD):
                blocks(bank[2 + m][:, :], lambda k: wk_s[:, k, m * P:(m + 1) * P], lambda k: qT[:, k, :])\
                    .then_inc(qk_done, 1)
            for t in range(T):
                ins = blocks(bank[0][:, t:t + 1], lambda k: qT[:, k, t * P:(t + 1) * P], lambda k: bk_s[:, k:k + 1])
            ins.then_inc(bkq_done, 1)
            pe.wait_ge(qkT_ok, KD)
            pe.wait_ge(bkq_ok, 1)

            def scores(i, n):
                hold(pe, ctxT_in[n], i * 16 + 16)
                for k in range(KD):
                    for a_ in range(2):
                        ins = mm(psum[a_ * S:(a_ + 1) * S, n * 512:n * 512 + NCOLS[n]], qp[:, k, a_ * S:(a_ + 1) * S],
                                 ctxT[n][:, a_, k, :], start=(k == 0), stop=(k == KD - 1))
                ins.then_inc(sc_done, 1)

            def turn_exps(i):
                hold(pe, exp_ok, i + 1)
                for n in range(NC):
                    for j in range(4 * n, min(4 * n + 4, J)):
                        w_ = REST if j == JF else P
                        ins = tr(bank[n][0:w_, (j % 4) * P:(j % 4 + 1) * P], pr[:, j * P:j * P + w_])
                    ins.then_inc(prt_done, 1)

            def weigh(i, js):
                for j in js:
                    if j == 0:
                        hold(pe, ctx_in_s, i * 64 + 64)
                    if j % 4 == 0:
                        hold(pe, prT_ok, i * NC + (j // 4 + 1))
                    w_ = REST if j == JF else P
                    for a_ in range(2):
                        ins = mm(bank[4][a_ * S:(a_ + 1) * S, :], prT[0:w_, j, a_ * S:(a_ + 1) * S], ctx[a_][0:w_, j, :],
                                 start=(j == 0), stop=(j == J - 1))
                    if j == J - 1:
                        ins.then_inc(av_done, 1)

            def turn(dst, src, ok, n, done):
                hold(pe, ok, n)
                for k in range(KD):
                    ins = tr(dst[:, k * P:(k + 1) * P], src[:, k * P:(k + 1) * P])
                ins.then_inc(done, 1)

            def project(dst, lhsT, w_, ok, n, done):
                hold(pe, ok, n)
                blocks(dst, lambda k: lhsT[:, k, :], lambda k: w_[:, k, :]).then_inc(done, 1)

            def fold_projections():
                pe.wait_ge(wvo_in, 32)
                pe.wait_ge(bv_ok, 1)
                blocks(bank[7], lambda k: bv_w[:, k, :], lambda k: wo_s[:, k, :]).then_inc(bvo_done, 1)
                for m in range(KD):
                    if m == KD - 1:
                        pe.wait_ge(bo_ok, 1)
                    blocks(bank[4 + m], lambda k: wv_s[:, k, m * P:(m + 1) * P], lambda k: wo_s[:, k, :]).then_inc(wvo_done, 1)

            def turn_x2(t):
                turn(bank[t], xn[:, t, :], xn2_ok, t + 1, x2t_done)

            def logits(t):
                pe.wait_ge(xT_ok, t + 1)
                blocks(bank[4][:, t * E:(t + 1) * E], lambda k: x2T[:, k, t * P:(t + 1) * P], lambda k: rw_s[:, k, :])\
                    .then_inc(lg_done, 1)

            def step_bc(i, b, c):
                t = i - 1
                if b:
                    hold(pe, qp_ok, i + 1)
                    scores(i, 0)
                else:
                    turn_x2(0)
                if c:
                    project(bank[7], aT, wvo, aT_ok, t + 1, o_done)
                if b:
                    scores(i, 1)
                    scores(i, 2)
                else:
                    turn_x2(1)
                    turn_x2(2)
                    logits(0)
                if c:
                    hold(pe, y_free, t + 1)
                    turn(bank[5], h_nat, h_ok, t + 1, ht_done)
                if b:
                    scores(i, 3)
                else:
                    logits(1)
                    logits(2)
                if c:
                    project(bank[7], hT, wr_s, hT_ok, t + 1, fr_done)
                    blocks(bank[6], lambda k: hT[:, k, :], lambda k: wl_s[:, k, :]).then_inc(fl_done, 1)
                else:
                    fold_projections()
                if b:
                    turn_exps(i)
                if not c:
                    pe.wait_ge(wvo_ok, KD)
                if c:
                    hold(pe, sr_ok, t + 1)
                    tr(bank[5][0:H, 0:P], sr).then_inc(srT_done, 1)
                if b:
                    weigh(i, range(0, 2))
                if c:
                    hold(pe, mxl_ok, t + 1)
                    mm(bank[5][:, 256:256 + H], mxl[0:H, :], ident[0:H, 0:H], start=True, stop=True).then_inc(srm_done, 1)
                if b:
                    weigh(i, range(2, 5))
                if c:
                    hold(pe, spread_ok, t + 1)
                    for n in range(2):
                        ins = mm(bank[6 + n], same, wide[n], start=True, stop=True)
                    ins.then_inc(st_done, 1)
                if b:
                    weigh(i, range(5, 8))
                if c:
                    hold(pe, pexp_ok, t + 1)
                    for h in range(H):
                        for b_ in range(2):
                            n = h % 4 * (HD + 1)
                            ins = mm(bank[6 + h // 4][b_ * S:(b_ + 1) * S, n:n + HD + 1], att_p[b_ * S:(b_ + 1) * S, h * S:(h + 1) * S],
                                     fr[b_ * S:(b_ + 1) * S, h, :], start=True, stop=True)
                    ins.then_inc(hs_done, 1)
                if b:
                    weigh(i, range(8, 10))
                if c:
                    turn(bank[5], hs_nat, hn_ok, t + 1, hst_done)
                if b:
                    weigh(i, range(10, J))
                if c:
                    project(bank[5], hsT, wf_s, hsT_ok, t + 1, wf_done)
                if b:
                    turn(bank[7], ao, ao_ok, i + 1, at_done)

            step_bc(0, True, False)
            pe.wait_ge(const_ok, 1)
            pe.wait_ge(wc_in, 16 * 3)
            with pe.Fori(1, PAIRS) as i:
                step_bc(i, True, True)
            step_bc(PAIRS, False, True)
            turn_x2(T - 1)
            logits(T - 1)
            pe.wait_ge(hot_ok, 1)
            flat = both.rearrange("p t e -> p (t e)")
            mm(bank[5][:, 0:(T + 1) * E], below, flat, start=True, stop=False)
            for u in range(1, T + 1):
                ins = mm(bank[5][:, u * E:(T + 1) * E], ones, flat[:, 0:(T + 1 - u) * E], start=False, stop=(u == T))
            ins.then_inc(rank_done, 1)

            def turn_rows(arrived, n):
                hold(pe, arrived, n)
                for k in range(KD):
                    ins = tr(bank[7][:, k * W:(k + 1) * W], xg[:, k * P:(k + 1) * P], W)
                ins.then_inc(xgt_done, 1)

            def up(r, q):
                for k in range(KD):
                    for a_ in range(2):
                        ins = mm(bank[q][a_ * W:(a_ + 1) * W, :], xgT[:, k, :], w1buf[r][:, q, a_, k, :],
                                 start=(k == 0), stop=(k == KD - 1))
                ins.then_inc(up_done, 1)

            def turn_hidden(c, u):
                pe.wait_ge(hid_ok, c * 2 + (u + 1))
                for n in range(4):
                    ins = tr(bank[5 + u][:, n * P:(n + 1) * P], hid[u][:, n * P:(n + 1) * P])
                ins.then_inc(hidt_done, 1)

            def down(u, n):
                for a_ in range(2):
                    ins = mm(bank[4][a_ * W:(a_ + 1) * W, :], hidT[:, u, n, a_ * W:(a_ + 1) * W],
                             w2buf[:, (u * 4 + n) * 2 + a_, :], start=(u == 0 and n == 0), stop=(u == 1 and n == 3))
                if u == 1 and n == 3:
                    ins.then_inc(down_done, 1)

            turn_rows(xg_in, 16)
            with pe.Fori(0, E // 2) as ep:
                for r in range(2):
                    lo, hi = chunk_range(pe, ep * 2 + r)
                    with pe.Fori(lo, hi) as c:
                        hold(pe, xgT_ok, c + 1)
                        for q in range(PIECES):
                            hold(pe, w1_in[r][q], ep * 16 + 16)
                            up(r, q)
                            if q == 2:
                                turn_hidden(c, 0)
                        hold(pe, w2_in[0], ep * 32 + (16 * r + 16))
                        hold(pe, hidT_ok, c * 2 + 1)
                        for n in range(4):
                            down(0, n)
                            if n == 2:
                                turn_hidden(c, 1)
                        turn_rows(xg_ok, c + 1)
                        hold(pe, w2_in[1], ep * 32 + (16 * r + 16))
                        hold(pe, hidT_ok, c * 2 + 2)
                        for n in range(4):
                            down(1, n)

        @block.vector
        def _(dve):
            v = nc.vector
            o = Order(dve, v_order)

            def norm_stats(kind, col, src, oc):
                dve.sem_inc(passed[dve.engine], 1)
                oc.link(v.bn_stats(stats[:, col, :], src))
                dve.sem_inc(passed[dve.engine], 1)
                oc.link(v.bn_aggr(mv[:, col, :], stats[:, col, :]))
                v.tensor_scalar(mv[:, col, 1:2], mv[:, col, 1:2], EPS, None, ALU.add).then_inc(var_ok[kind], 1)

            def normalise(kind, n, col, dst, src):
                dve.wait_ge(rstd_ok[kind], n + 1)
                return v.tensor_scalar(dst, src, mv[:, col, 0:1], rstd[:, col:col + 1], ALU.subtract, ALU.mult)

            for t in range(T):
                dve.wait_ge(x_in[t], 16)
                norm_stats(0, t, xres[:, t, :], o)
                if t:
                    normalise(0, t - 1, t - 1, xn[:, t - 1, :], xres[:, t - 1, :]).then_inc(xn_ok, 1)
            normalise(0, T - 1, T - 1, xn[:, T - 1, :], xres[:, T - 1, :]).then_inc(xn_ok, 1)

            def tile_rows(ap, t):
                return ap[:, bass.ds(t, 1), :].rearrange("p o d -> p (o d)")

            def row_max(i):
                ob = Order(dve, row_order, i * 3)
                ob.link(v.tensor_copy(bkq1, bkq[:, bass.ds(i, 1)]))
                hold(dve, sc_done, i * NC + NC)
                ob.link(v.tensor_reduce(mx, psum[:, 0:KEYS], AX.X, ALU.max))
                ob.link(v.tensor_tensor(mxr, mx, bkq1, ALU.add))
                v.tensor_scalar(nb, bkq1, mxr, SCALE, ALU.subtract, ALU.mult).then_inc(nb_ok, 1)

            def row_recip(i):
                dve.wait_ge(exp_ok, i + 1)
                v.reciprocal(rec, den).then_inc(rec_ok, 1)

            def attended(i):
                hold(dve, av_done, i + 1)
                hold(dve, rec_ok, i + 1)
                v.tensor_scalar(ao, bank[4], rec, None, ALU.mult).then_inc(ao_ok, 1)

            def add_cross(t):
                on = Order(dve, n_order, t * 13)
                hold(dve, o_done, t + 1)
                rows = tile_rows(xres, t)
                on.link(v.tensor_tensor(rows, bank[7], rows, ALU.add))
                norm_stats(1, 1, rows, on)
                normalise(1, t, 1, h_nat, rows).then_inc(h_ok, 1)

            def by_head(ap):
                return ap.rearrange("p (h d) -> p h d", h=H)

            def right(t):
                os_ = Order(dve, side_order, t * 10)
                th = by_head(wide[1])
                dve.wait_ge(fr_ok, t + 1)
                os_.link(v.scalar_tensor_tensor(out=th, in0=fr[:, :, 0:HD], scalar=0.01, in1=fr[:, :, 0:HD], op0=ALU.mult, op1=ALU.max))
                os_.link(v.tensor_tensor(th, th, attr_s.unsqueeze(1).to_broadcast([P, H, HD]), ALU.mult))
                v.tensor_reduce(sr, th, AX.X, ALU.add).then_inc(sr_ok, 1)

            def left(t):
                os_ = Order(dve, side_order, t * 10 + 2)
                tmp, th = wide[0], by_head(wide[0])
                dve.wait_ge(fl_done, t + 1)
                os_.link(v.tensor_scalar(tmp, bank[6], 0.01, None, ALU.mult))
                os_.link(v.tensor_tensor(tmp, bank[6], tmp, ALU.max))
                dve.wait_ge(srT_done, t + 1)
                os_.link(v.tensor_reduce(srx[0:H, :], bank[5][0:H, 0:P].rearrange("h (b m) -> h b m", b=2), AX.X, ALU.max))
                v.tensor_copy(mxl[0:H, :].rearrange("h (b m) -> h b m", b=2),
                              srx[0:H, :].unsqueeze(2).to_broadcast([H, 2, S])).then_inc(mxl_ok, 1)
                os_.link(v.tensor_tensor(th, th, attl_s.unsqueeze(1).to_broadcast([P, H, HD]), ALU.mult))
                os_.link(v.tensor_reduce(sl, th, AX.X, ALU.add))

            def spread_left(t):
                os_ = Order(dve, side_order, t * 10 + 7)
                dve.wait_ge(srm_done, t + 1)
                os_.link(v.tensor_tensor(slm, sl, bank[5][:, 256:256 + H], ALU.add))
                mask = place.unsqueeze(1).to_broadcast([P, H, S])
                os_.link(v.tensor_tensor(wide[0].rearrange("p (h n) -> p h n", h=H), sl.unsqueeze(2).to_broadcast([P, H, S]), mask, ALU.mult))
                v.tensor_tensor(wide[1].rearrange("p (h n) -> p h n", h=H), slm.unsqueeze(2).to_broadcast([P, H, S]), mask, ALU.mult)\
                    .then_inc(spread_ok, 1)

            def exponents(t):
                os_ = Order(dve, side_order, t * 10 + 9)
                dve.wait_ge(st_done, t + 1)
                os_.link(v.tensor_tensor(att_p.rearrange("p (h n) -> p h n", h=H), bank[6].rearrange("p (h n) -> p h n", h=H),
                                         sr.unsqueeze(2).to_broadcast([P, H, S]), ALU.add))
                v.tensor_tensor(att_p, att_p, bank[7], ALU.subtract).then_inc(arg_ok, 1)

            def shares(t):
                on = Order(dve, n_order, t * 13 + 3)
                dve.wait_ge(hs_done, t + 1)
                sums = [bank[6 + n][:, 0:4 * (HD + 1)].rearrange("p (h d) -> p h d", h=4) for n in range(2)]
                for n in range(2):
                    on.link(v.reciprocal(hden[:, 4 * n:4 * n + 4].unsqueeze(2), sums[n][:, :, HD:HD + 1]))
                to = hs_nat.rearrange("p (h d) -> p h d", h=H)
                for n in range(2):
                    ins = v.tensor_tensor(to[:, 4 * n:4 * n + 4, :], sums[n][:, :, 0:HD],
                                          hden[:, 4 * n:4 * n + 4].unsqueeze(2).to_broadcast([P, 4, HD]), ALU.mult)
                    if n:
                        ins.then_inc(hn_ok, 1)
                    else:
                        on.link(ins)

            def add_self(t):
                on = Order(dve, n_order, t * 13 + 6)
                dve.wait_ge(wf_done, t + 1)
                on.link(v.tensor_tensor(yn, bank[5], h_nat, ALU.add))
                dve.sem_inc(y_free, 1)
                norm_stats(2, 2, yn, on)
                on.link(v.scalar_tensor_tensor(out=yn, in0=yn, scalar=mv[:, 2, 0:1], in1=gamma_s, op0=ALU.subtract, op1=ALU.mult))
                rows = tile_rows(xres, t)
                hold(dve, x1b_ok, t + 1)
                hold(dve, rstd_ok[2], t + 1)
                on.link(v.scalar_tensor_tensor(out=rows, in0=yn, scalar=rstd[:, 2:3], in1=rows, op0=ALU.mult, op1=ALU.add))
                norm_stats(3, 3, rows, on)
                normalise(3, t, 3, tile_rows(xn, t), rows).then_inc(xn2_ok, 1)

            dve.wait_ge(bkq_ok, 1)
            dve.wait_ge(small_in, 16 * 7)
            dve.sem_inc(y_free, 1)
            dve.wait_ge(bo_in, 16)
            dve.wait_ge(bvo_done, 1)
            v.tensor_tensor(bo_s, bank[7], bo_s, ALU.add).then_inc(bo_ok, 1)
            row_max(0)
            row_recip(0)
            attended(0)
            dve.wait_ge(xb_ok, T)
            dve.wait_ge(gb_in, 32)
            with dve.Fori(1, PAIRS) as i:
                t = i - 1
                add_cross(t)
                row_max(i)
                row_recip(i)
                right(t)
                left(t)
                spread_left(t)
                exponents(t)
                shares(t)
                attended(i)
                add_self(t)
            t = PAIRS - 1
            add_cross(t)
            right(t)
            left(t)
            spread_left(t)
            exponents(t)
            shares(t)
            add_self(t)

            v.memset(both[:, T, :], 0.0)
            dve.wait_ge(lg_done, T)
            wideE = lambda ap: ap.unsqueeze(2).to_broadcast([P, T, E])
            wideT = lambda ap: ap.unsqueeze(1).to_broadcast([P, T, E])
            o.link(v.tensor_tensor(lg, bank[4][:, 0:T * E].rearrange("p (t e) -> p t e", t=T), wideT(rb_s), ALU.add))

            def pick(src, best, hot_):
                o.link(v.tensor_reduce(best, src, AX.X, ALU.max))
                o.link(v.tensor_tensor(eq, src, wideE(best), ALU.is_equal))
                o.link(v.scalar_tensor_tensor(out=cand, in0=eq, scalar=-2.0 * E, in1=wideT(iota2), op0=ALU.mult, op1=ALU.add))
                o.link(v.tensor_reduce(idx, cand, AX.X, ALU.min))
                o.link(v.tensor_tensor(hot_, wideT(iota), wideE(idx), ALU.is_equal))

            pick(lg, top[:, 0, :], hot[:, 0, :, :])
            o.link(v.scalar_tensor_tensor(out=lg2, in0=hot[:, 0, :, :], scalar=LOWEST, in1=lg, op0=ALU.mult, op1=ALU.add))
            pick(lg2, top[:, 1, :], hot[:, 1, :, :])
            v.tensor_tensor(both[:, 0:T, :], hot[:, 0, :, :], hot[:, 1, :, :], ALU.add).then_inc(hot_ok, 1)
            v.tensor_tensor(ew, top[:, 1, :], top[:, 0, :], ALU.subtract).then_inc(top_ok, 1)
            dve.wait_ge(rank_done, 1)
            o.link(v.tensor_tensor(cmp8, bank[5][:, T * E:(T + 1) * E].unsqueeze(2).to_broadcast([P, E, E]),
                                   over.unsqueeze(1).to_broadcast([P, E, E]), ALU.is_gt))
            o.link(v.tensor_reduce(chs, cmp8, AX.X, ALU.add))
            o.link(v.scalar_tensor_tensor(out=key, in0=chs, scalar=float(E), in1=early, op0=ALU.mult, op1=ALU.add))
            o.link(v.tensor_tensor(before, key.unsqueeze(1).to_broadcast([P, E, E]), key.unsqueeze(2).to_broadcast([P, E, E]), ALU.is_gt))
            o.link(v.tensor_tensor(cmp8, before, chs.unsqueeze(1).to_broadcast([P, E, E]), ALU.mult))
            o.link(v.tensor_reduce(first, cmp8, AX.X, ALU.add))
            o.link(v.scalar_tensor_tensor(out=rank, in0=wideT(first), scalar=float(W),
                                          in1=bank[5][:, 0:T * E].rearrange("p (t e) -> p t e", t=T), op0=ALU.mult, op1=ALU.add))
            o.link(v.tensor_tensor(cand2, hot, rank.unsqueeze(1).to_broadcast([P, 2, T, E]), ALU.mult))
            o.link(v.tensor_reduce(dst_f, cand2, AX.X, ALU.add))
            v.tensor_copy(dest_i[:, :, :], dst_f).then_inc(dest_ok, 1)
            o.link(v.tensor_reduce(pos, before, AX.X, ALU.add))
            o.link(v.tensor_tensor(cmp9, pos.unsqueeze(1).to_broadcast([P, E + 1, E]), count9.unsqueeze(2).to_broadcast([P, E + 1, E]), ALU.is_lt))
            o.link(v.tensor_tensor(cmp9, cmp9, chs.unsqueeze(1).to_broadcast([P, E + 1, E]), ALU.mult))
            o.link(v.tensor_reduce(basef[:, 0, :], cmp9, AX.X, ALU.add))
            o.link(v.tensor_tensor(cmp9, pos.unsqueeze(1).to_broadcast([P, E + 1, E]), count9.unsqueeze(2).to_broadcast([P, E + 1, E]), ALU.is_equal))
            o.link(v.tensor_tensor(cmp9, cmp9, iota.unsqueeze(1).to_broadcast([P, E + 1, E]), ALU.mult))
            o.link(v.tensor_reduce(basef[:, 2, :], cmp9, AX.X, ALU.add))
            o.link(v.tensor_scalar(basef[:, 1, :], basef[:, 0, :], -1.0, None, ALU.add))
            v.tensor_copy(base_i[:, :, :], basef).then_inc(base_ok, 1)
            dve.wait_ge(ew_ok, 1)
            o.link(v.tensor_scalar(wsum, ew, 1.0, None, ALU.add))
            o.link(v.reciprocal(gate[:, 0, :], wsum))
            v.tensor_tensor(gate[:, 1, :], gate[:, 0, :], ew, ALU.mult).then_inc(gate_ok, 1)

            dve.wait_ge(xgt_done, 1)
            dve.wait_ge(dest_ok, 1)
            dve.wait_ge(gate_ok, 1)
            turned_rows = bank[7][:, 0:KD * W].rearrange("p (k c) -> p k c", k=KD)
            v.tensor_copy(xgT, turned_rows).then_inc(xgT_ok, 1)
            with dve.Fori(0, E // 2) as ep:
                for r in range(2):
                    lo, hi = chunk_range(dve, ep * 2 + r)
                    hold(dve, bias_in[r], ep * 48 + 48)
                    with dve.Fori(lo, hi) as c:
                        oc = Order(dve, sum_order, c * 3)
                        for u in range(2):
                            hold(dve, up_done, c * PIECES + (2 * u + 1))
                            v.tensor_tensor(glu[u], bank[2 * u][:, :], b1_s[r][:, 2 * u, :], ALU.add).then_inc(lin_ok, 1)
                            hold(dve, up_done, c * PIECES + (2 * u + 2))
                            oc.link(v.tensor_tensor(hid[u], bank[2 * u + 1][:, :], b1_s[r][:, 2 * u + 1, :], ALU.add))
                            dve.wait_ge(silu_ok, c * 2 + (u + 1))
                            v.tensor_tensor(hid[u], hid[u], glu[u], ALU.mult).then_inc(hid_ok, 1)
                        dve.wait_ge(xgt_done, c + 2)
                        v.tensor_copy(xgT, turned_rows).then_inc(xgT_ok, 1)
                        dve.wait_ge(y_stored, c * 16 + 16)
                        hold(dve, down_done, c + 1)
                        oc.link(v.tensor_tensor(yrow, bank[4][0:W, :], b2_s[r], ALU.add))
                        v.tensor_tensor(yrow, bank[4][W:P, :], yrow, ALU.add).then_inc(yrow_ok, 1)
            for t in range(T):
                dve.wait_ge(got_in[t], 32)
                for k in range(2):
                    v.scalar_tensor_tensor(out=xres[:, t, :], in0=got[:, k, t, :], scalar=gate[:, k, t:t + 1],
                                           in1=xres[:, t, :], op0=ALU.mult, op1=ALU.add).then_inc(res_ok, 1)
                    if k == 0:
                        dve.wait_ge(res_ok, 2 * t + 1)


def kernel(**inputs):
    import numpy as np
    import concourse.bacc as bacc
    from concourse.bass_utils import run_bass_kernel_spmd

    a = {k: np.asarray(v) for k, v in inputs.items()}

    def cols(vec):
        return vec.reshape(-1, P).T

    def rows_of(mat):
        return mat.reshape(-1, P, mat.shape[1]).transpose(1, 0, 2)

    w1 = a["L0_ffn_w1"].reshape(E, 2, 2, 2, 512, KD, P)
    b1 = a["L0_ffn_b1"].reshape(E, 2, 2, 2, 512)
    w2 = a["L0_ffn_w2"].reshape(E, D, 2, 2, 4, P)
    c = a["ctx_1024"]
    head = c[:, :JF * P].reshape(B, P, JF, D).transpose(0, 3, 2, 1).reshape(B, D, JF * P)
    cT = np.concatenate([head, c[:, JF * P:].transpose(0, 2, 1)], axis=2).reshape(PAIRS, 2, KD, P, KEYS)
    cT = cT.transpose(0, 3, 1, 2, 4)
    cT = np.concatenate([cT[..., n * 512:n * 512 + NCOLS[n]].reshape(PAIRS, P, -1) for n in range(NC)], axis=2)
    arrays = {
        "x": a["x"].reshape(TOK, D),
        "ctx": a["ctx_1024"],
        "ctxT": cT,
        "wq": rows_of(a["L0_xattn_Wq"].T), "bq": cols(a["L0_xattn_bq"]),
        "wk": rows_of(a["L0_xattn_Wk"]), "bk": cols(a["L0_xattn_bk"]),
        "wv": rows_of(a["L0_xattn_Wv"]), "bv": cols(a["L0_xattn_bv"]),
        "wo": rows_of(a["L0_xattn_Wo"].T), "bo": a["L0_xattn_bo"],
        "wl": rows_of(a["L0_attn_Wl"].T), "wr": rows_of(a["L0_attn_Wr"].T),
        "att_l": a["L0_attn_att_l"].reshape(HD), "att_r": a["L0_attn_att_r"].reshape(HD),
        "wf": rows_of(a["L0_attn_Wf"].T), "gamma": a["L0_attn_ln_gamma"], "beta": a["L0_attn_ln_beta"],
        "rw": rows_of(a["L0_ffn_router_w"].T), "rb": a["L0_ffn_router_b"],
        "w1": w1.transpose(0, 6, 3, 1, 2, 5, 4).reshape(E, P, PIECES * 2 * KD * 512),
        "b1": b1.transpose(0, 2, 3, 1, 4).reshape(E, 2, PIECES * 512),
        "w2": w2.transpose(0, 5, 3, 4, 2, 1).reshape(E, P, M2 * D),
        "b2": a["L0_ffn_b2"],
    }
    nc = bacc.Bacc("TRN2", target_bir_lowering=False, num_devices=1)
    ins, args = {}, []
    for name, arr in arrays.items():
        arr = np.ascontiguousarray(arr)
        ins[f"in_{name}"] = arr
        args.append(nc.dram_tensor(f"in_{name}", arr.shape, mybir.dt.from_np(arr.dtype), kind="ExternalInput").ap())
    args.append(nc.dram_tensor("out", (TOK, D), F32, kind="ExternalOutput").ap())
    perceiver_layer(nc, *args)
    r = run_bass_kernel_spmd(nc, [ins], core_ids=[0])
    return r.results[0]["out"].reshape(B, S, D)
```
